# Optimizing a Trainium2 kernel written in Bass

```python
import numpy as np
import jax
import jax.numpy as jnp

def _softmax(x, axis=-1):
    return jax.nn.softmax(x, axis=axis)

def _gelu(x):
    return jax.nn.gelu(x, approximate=True)

def _silu(x):
    return jax.nn.silu(x)

def _sigmoid(x):
    return jax.nn.sigmoid(x)

def _layernorm(x, axis=-1, eps=1e-05):
    m = jnp.mean(x, axis=axis, keepdims=True)
    v = jnp.var(x, axis=axis, keepdims=True)
    return (x - m) / jnp.sqrt(v + eps)

def _scatter_add(tgt, idx, src, axis=0):
    return tgt.at[idx].add(src)

def _segment_sum(src, seg, n):
    return jax.ops.segment_sum(src, seg, n)
kernel_name = 'mk_seq_postln_d1_jaxref_r8_35eac2'

def setup_inputs(seed: int=0):
    np.random.seed(seed)
    _w = jnp.asarray

    def _L0_attn_setup():
        import jax, jax.numpy as jnp
        import numpy as np
        B, L, D, H = (2, 256, 256, 16)
        HD = D // H

        def rope(x, seq_len, theta=10000.0):
            d = x.shape[-1]
            freqs = 1.0 / theta ** (jnp.arange(0, d, 2, dtype=x.dtype) / d)
            t = jnp.arange(seq_len, dtype=x.dtype)
            f = jnp.outer(t, freqs)
            sin = jnp.repeat(jnp.sin(f), 2, axis=-1)
            cos = jnp.repeat(jnp.cos(f), 2, axis=-1)
            x1, x2 = (x[..., ::2], x[..., 1::2])
            x_rot = jnp.stack([-x2, x1], axis=-1).reshape(x.shape)
            return x * cos + x_rot * sin
        key = jax.random.key(seed)
        k1, k2, k3 = jax.random.split(key, 3)
        x = jax.random.normal(k1, (B, L, D), dtype=jnp.float32)
        w_qkv = jax.random.normal(k2, (D, 3 * D), dtype=jnp.float32) * (1.0 / np.sqrt(D))
        w_proj = jax.random.normal(k3, (D, D), dtype=jnp.float32) * (1.0 / np.sqrt(D))
        return {'x': x, 'w_qkv': w_qkv, 'w_proj': w_proj}
    _L0_attn_in = _L0_attn_setup()

    def _L0_ffn_setup():
        import jax, jax.numpy as jnp
        import numpy as np
        B, S, H = (1, 128, 256)
        F = 128
        E = 16
        K = 2
        NS = 1
        ROUTE_SCALE = 1.0
        key = jax.random.key(seed)
        ks = jax.random.split(key, 8)

        def w(k, shape, fan_in):
            return jax.random.normal(k, shape, jnp.float32) * fan_in ** (-0.5)
        return {'hidden_states': jax.random.normal(ks[0], (B, S, H), jnp.float32), 'gate_w': w(ks[1], (H, E), H), 'expert_bias': jnp.zeros((E,), jnp.float32), 'shared_gate_w': w(ks[2], (H, F * NS), H), 'shared_up_w': w(ks[3], (H, F * NS), H), 'shared_down_w': w(ks[4], (F * NS, H), F * NS), 'experts_gate_up': w(ks[5], (E, H, 2 * F), H), 'experts_down': w(ks[6], (E, F, H), F)}
    _L0_ffn_in = _L0_ffn_setup()
    _d = {'L0_attn_x': _L0_attn_in['x'], 'L0_attn_w_qkv': _L0_attn_in['w_qkv'], 'L0_attn_w_proj': _L0_attn_in['w_proj'], 'L0_ffn_gate_w': _L0_ffn_in['gate_w'], 'L0_ffn_expert_bias': _L0_ffn_in['expert_bias'], 'L0_ffn_shared_gate_w': _L0_ffn_in['shared_gate_w'], 'L0_ffn_shared_up_w': _L0_ffn_in['shared_up_w'], 'L0_ffn_shared_down_w': _L0_ffn_in['shared_down_w'], 'L0_ffn_experts_gate_up': _L0_ffn_in['experts_gate_up'], 'L0_ffn_experts_down': _L0_ffn_in['experts_down']}
    _x0 = _d['L0_attn_x']
    _d['L0_attn_x'] = jax.random.normal(jax.random.fold_in(jax.random.key(seed), 1), (4, 1024, 256), dtype=_x0.dtype)
    del _x0
    return _d

def reference(L0_attn_x, L0_attn_w_qkv, L0_attn_w_proj, L0_ffn_gate_w, L0_ffn_expert_bias, L0_ffn_shared_gate_w, L0_ffn_shared_up_w, L0_ffn_shared_down_w, L0_ffn_experts_gate_up, L0_ffn_experts_down):

    def _L0_attn_ref(x, w_qkv, w_proj):
        import jax, jax.numpy as jnp
        import numpy as np
        B, L, D, H = (2, 256, 256, 16)
        HD = D // H

        def rope(x, seq_len, theta=10000.0):
            d = x.shape[-1]
            freqs = 1.0 / theta ** (jnp.arange(0, d, 2, dtype=x.dtype) / d)
            t = jnp.arange(seq_len, dtype=x.dtype)
            f = jnp.outer(t, freqs)
            sin = jnp.repeat(jnp.sin(f), 2, axis=-1)
            cos = jnp.repeat(jnp.cos(f), 2, axis=-1)
            x1, x2 = (x[..., ::2], x[..., 1::2])
            x_rot = jnp.stack([-x2, x1], axis=-1).reshape(x.shape)
            return x * cos + x_rot * sin
        Bc, Lc, Dc = x.shape
        scale = 1.0 / np.sqrt(HD)
        qkv = (x @ w_qkv).reshape(Bc, Lc, 3, H, HD)
        q, k, v = (qkv[:, :, 0], qkv[:, :, 1], qkv[:, :, 2])
        q = rope(jnp.transpose(q, (0, 2, 1, 3)), Lc)
        k = rope(jnp.transpose(k, (0, 2, 1, 3)), Lc)
        v = jnp.transpose(v, (0, 2, 1, 3))
        att = jnp.einsum('bhqd,bhkd->bhqk', q, k) * scale
        att = jax.nn.softmax(att, axis=-1)
        out = jnp.einsum('bhqk,bhkd->bhqd', att, v)
        out = jnp.transpose(out, (0, 2, 1, 3)).reshape(Bc, Lc, Dc)
        return out @ w_proj

    def _L0_ffn_ref(hidden_states, gate_w, expert_bias, shared_gate_w, shared_up_w, shared_down_w, experts_gate_up, experts_down):
        import jax, jax.numpy as jnp
        import numpy as np
        B, S, H = (1, 128, 256)
        F = 128
        E = 16
        K = 2
        NS = 1
        ROUTE_SCALE = 1.0
        b, s, h = hidden_states.shape
        x = hidden_states.reshape(-1, h)
        T = x.shape[0]
        router_logits = (x @ gate_w).astype(jnp.float32)
        scores = jax.nn.sigmoid(router_logits)
        _, selected = jax.lax.top_k(scores + expert_bias[None, :], K)
        top_scores = jnp.take_along_axis(scores, selected, axis=1)
        top_scores = top_scores / (top_scores.sum(-1, keepdims=True) + 1e-20)
        top_scores = top_scores * ROUTE_SCALE
        shared = jax.nn.silu(x @ shared_gate_w) * (x @ shared_up_w) @ shared_down_w
        comb = jnp.zeros((T, E), jnp.float32).at[jnp.arange(T)[:, None], selected].add(top_scores)
        routed = jnp.zeros_like(x)
        for e in range(E):
            gu = x @ experts_gate_up[e]
            g, u = jnp.split(gu, 2, axis=-1)
            routed = routed + comb[:, e:e + 1] * (jax.nn.silu(g) * u @ experts_down[e])
        return (shared + routed).reshape(b, s, h)
    x = L0_attn_x
    x = _layernorm(x + _L0_attn_ref(x, L0_attn_w_qkv, L0_attn_w_proj), axis=-1)
    x = _layernorm(x + _L0_ffn_ref(x, L0_ffn_gate_w, L0_ffn_expert_bias, L0_ffn_shared_gate_w, L0_ffn_shared_up_w, L0_ffn_shared_down_w, L0_ffn_experts_gate_up, L0_ffn_experts_down), axis=-1)
    return x

_drawn_inputs = setup_inputs


def setup_inputs(seed=0):
    import zlib

    import numpy as np

    out = dict(_drawn_inputs(seed))
    spreads = {'L0_ffn_expert_bias': (0.0, 0.1)}
    factors = {}
    for name, (base, spread) in spreads.items():
        noise = np.random.default_rng([zlib.crc32(name.encode()), seed]).standard_normal(out[name].shape)
        drawn = base * np.exp(spread * noise) if base else spread * noise
        out[name] = jnp.asarray(drawn.astype(out[name].dtype))
    for name, factor in factors.items():
        out[name] = (out[name] * factor).astype(out[name].dtype)
    return out
```

```python
import math
from contextlib import ExitStack

import concourse.bass as bass
from concourse import mybir

P = 128
B, L, D, HEADS, HD = 4, 1024, 256, 16, 16
T = B * L
EXPERTS, F = 16, 128
EPS = 1e-5

HG = 4
GROUPS = HEADS // HG
UNITS = B * GROUPS
KT = L // P
HALF = 512
STEPS = KT * (L // HALF)
LEAD = 12
CUT = STEPS - LEAD - 1
PARTS = 3
SLOTS = 6
Q_SLOT = [0, 0, 1, 0, 1, 2]
K_SLOT = [0, 1, 0, 2, 1, 0]
ROWS = SLOTS * HD
M_ROWS = 2
VW = 32
SCALE = 1.0 / math.sqrt(HD)

ALU = mybir.AluOpType
ACT = mybir.ActivationFunctionType
AX = mybir.AxisListType
F32 = mybir.dt.float32
BF16 = mybir.dt.bfloat16
I32 = mybir.dt.int32
U32 = mybir.dt.uint32


def wait_apart(engine, constant, *waits):
    waits = [(semaphore, value if isinstance(value, int) else engine.to_reg(value)) for semaphore, value in waits]
    engine.wait_ge(*constant)
    for semaphore, value in waits:
        engine.wait_ge(semaphore, value)


def attention(nc, x_t, w_units, cos_t, sin_t, eye, parts_dram, attn, rows_dram):
    with ExitStack() as ctx:
        def sb(name, shape, dt=F32):
            return ctx.enter_context(nc.sbuf_tensor(name, shape, dt))

        def ps(name, shape, dt=F32):
            return ctx.enter_context(nc.psum_tensor(name, shape, dt))

        def sem(name):
            return ctx.enter_context(nc.semaphore(name))

        scores_ps = [ps(f"scores_ps{p}", [P, 2 * HALF]) for p in range(2)]
        rowmax_ps = [ps(f"rowmax_ps{p}", [P, HALF]) for p in range(2)]
        acc_ps = ps("acc_ps", [P, HALF])
        misc_ps = ps("misc_ps", [P, HALF])
        misc_bf = misc_ps[:, :].bitcast(BF16)

        eye_f = sb("eye_f", [P, P])
        eye_b = sb("eye_b", [P, P], BF16)
        cos_sb = sb("cos_sb", [P, L])
        sin_sb = sb("sin_sb", [P, L])
        xt_sb = sb("xt_sb", [P, 2, L])
        w_sb = sb("w_sb", [P, 2, 3 * HG * HD])
        raw = sb("raw", [P, 2, HALF])
        swapped = sb("swapped", [P, 2, HALF])
        term_c = sb("term_c", [P, HALF])
        term_s = sb("term_s", [P, HALF])
        roped = sb("roped", [P, 2, HALF])
        rest = sb("rest", [P, HALF])
        part = [sb(f"part{n}", [P, 2, HALF], BF16) for n in range(PARTS)]
        v_raw = sb("v_raw", [P, KT, HG, HD])
        v_sb = [sb(f"v_sb{p}", [P, KT, HG, VW]) for p in range(2)]
        q_st = [sb(f"q_st{p}", [ROWS + M_ROWS, 2, HG, HALF], BF16) for p in range(2)]
        k_st = [sb(f"k_st{p}", [ROWS + M_ROWS, HG, L], BF16) for p in range(2)]
        probs = [sb(f"probs{p}", [P, HG, HALF]) for p in range(2)]
        halfmax = sb("halfmax", [P, 4, HG, 2])
        negmax = sb("negmax", [P, HG, 4])
        negmax_parts = sb("negmax_parts", [P, M_ROWS, HG, 4], BF16)
        negmax_t = sb("negmax_t", [M_ROWS * HG * 4, P], BF16)
        acc_sb = sb("acc_sb", [P, HALF])
        recip = sb("recip", [P, 4, HG])
        zeros = sb("zeros", [P, 2560])

        zeros_set = sem("zeros_set")
        rows_cleared = sem("rows_cleared")
        consts = sem("consts")
        ones_set = sem("ones_set")
        w_loaded = sem("w_loaded")
        x_loaded = sem("x_loaded")
        qk_ready = sem("qk_ready")
        raw_copied = sem("raw_copied")
        v_ready = sem("v_ready")
        v_copied = sem("v_copied")
        v_placed = sem("v_placed")
        swap_done = sem("swap_done")
        terms_done = sem("terms_done")
        roped_done = sem("roped_done")
        hi_done = sem("hi_done")
        mid_done = sem("mid_done")
        lo_done = sem("lo_done")
        parts_out = [sem(f"parts_out{h}") for h in range(2)]
        k_loaded = sem("k_loaded")
        q_loaded = sem("q_loaded")
        rowmax_ready = sem("rowmax_ready")
        rowmax_read = sem("rowmax_read")
        negmax_step = sem("negmax_step")
        negmax_ready = sem("negmax_ready")
        negmax_turned = sem("negmax_turned")
        negmax_copied = sem("negmax_copied")
        negmax_placed = sem("negmax_placed")
        scores_ready = sem("scores_ready")
        probs_ready = sem("probs_ready")
        pv_done = sem("pv_done")
        acc_copied = sem("acc_copied")
        out_turned = sem("out_turned")
        recip_done = sem("recip_done")
        out_done = sem("out_done")

        block = ctx.enter_context(nc.Block())

        def units(engine, emit):
            emit(-1, 1, False, True, True)
            with engine.Fori(0, UNITS // 2 - 1) as pair:
                emit(pair * 2, 0, True, True, True)
                emit(pair * 2 + 1, 1, True, True, True)
            emit(UNITS - 2, 0, True, True, False)
            emit(UNITS - 1, 1, True, False, False)

        def step_of(u, par, s, this, next_):
            return (u, par, s, this) if s < STEPS else (u + 1, 1 - par, s - STEPS, next_)

        def maxima_of(u, par, s, this, next_):
            if s + LEAD < 2 * STEPS and s + LEAD - STEPS < 0:
                return (u, par, s + LEAD, this)
            m = s + LEAD - STEPS
            return (u, par, m, this) if m < 0 else (u + 1, 1 - par, m, next_) if m < STEPS else (u + 2, par, m - STEPS, False)

        @block.sync
        def _(sp):
            def load_w(v):
                sp.dma_start(w_sb[:, :, :], w_units[v % GROUPS].rearrange("(c p) n -> p c n", p=P)).then_inc(w_loaded, 16)

            def load_x(batch):
                sp.dma_start(xt_sb[:, :, :], x_t[batch].rearrange("(c p) t -> p c t", p=P)).then_inc(x_loaded, 16)

            def write_parts(v, h):
                sp.wait_ge(lo_done, v * 2 + h + 1)
                for n in range(PARTS):
                    sp.dma_start(parts_dram[v, 0, n, :, h].rearrange("d h t -> h d t"),
                                 part[n][0:HG * HD, h, :]).then_inc(parts_out[h], 16)
                    sp.dma_start(parts_dram[v, 1, n].rearrange("d a h t -> d (a h t)").rearrange("d (h a t) -> h d a t", a=2, t=HALF)[:, :, h],
                                 part[n][HG * HD:2 * HG * HD, h, :]).then_inc(parts_out[h], 16)

            def load_stacks(v, par):
                for h in range(2):
                    sp.wait_ge(parts_out[h], (v + 1) * (2 * PARTS * 16))
                for slot in range(SLOTS):
                    sp.dma_start(k_st[par][slot * HD:(slot + 1) * HD, :, :].rearrange("d h t -> d (h t)"),
                                 parts_dram[v, 1, K_SLOT[slot]].rearrange("d a h t -> d (a h t)")).then_inc(k_loaded, 16)
                for slot in range(SLOTS):
                    sp.dma_start(q_st[par][slot * HD:(slot + 1) * HD, :, :, :].rearrange("d a h t -> d (a h t)"),
                                 parts_dram[v, 0, Q_SLOT[slot]].rearrange("d a h t -> d (a h t)")).then_inc(q_loaded, 16)

            def place_negmax(v, par, h):
                sp.wait_ge(negmax_copied, v * 2 + h + 1)
                for r in range(M_ROWS):
                    sp.dma_start(q_st[par][ROWS + r:ROWS + r + 1, h, :, :].rearrange("o g (q t) -> o (g q) t", t=P),
                                 negmax_t[r * HG * 4:(r + 1) * HG * 4, :]).then_inc(negmax_placed, 16)

            def unit(u, par, this, next_, after):
                if this:
                    place_negmax(u, par, 1)
                if after:
                    write_parts(u + 2, 0)
                    write_parts(u + 2, 1)
                    sp.wait_ge(v_ready, u + 3)
                    load_w(u + 3)
                    if par:
                        load_x((u + 3) // GROUPS % B)
                if next_:
                    place_negmax(u + 1, 1 - par, 0)
                if after:
                    if this:
                        wait_apart(sp, (consts, 3 * 16), (scores_ready, (u + 1) * (2 * STEPS)))
                    load_stacks(u + 2, par)

            sp.dma_start(eye_f[:, :], eye).then_inc(consts, 16)
            load_w(0)
            load_x(0)
            sp.dma_start(cos_sb[:, :], cos_t).then_inc(consts, 16)
            sp.dma_start(sin_sb[:, :], sin_t).then_inc(consts, 16)
            write_parts(0, 0)
            write_parts(0, 1)
            sp.wait_ge(v_ready, 1)
            load_w(1)
            load_stacks(0, 0)
            units(sp, unit)
            sp.wait_ge(w_loaded, (UNITS + 1) * 16)
            sp.wait_ge(x_loaded, (UNITS // 2 + 1) * 16)

        @block.tensor
        def _(pe):
            def project_qk(v, pair, h):
                pe.wait_ge(w_loaded, (v + 1) * 16)
                pe.wait_ge(x_loaded, (pair + 1) * 16)
                for c in range(2):
                    last = nc.tensor.matmul(misc_ps[:, :], w_sb[:, c, 0:2 * HG * HD], xt_sb[:, c, h * HALF:(h + 1) * HALF],
                                            start=(c == 0), stop=(c == 1))
                last.then_inc(qk_ready, 1)

            def project_v(v):
                for t in range(KT):
                    for c in range(2):
                        last = nc.tensor.matmul(misc_ps[:, t * HG * HD:(t + 1) * HG * HD], xt_sb[:, c, t * P:(t + 1) * P],
                                                w_sb[:, c, 2 * HG * HD:3 * HG * HD], start=(c == 0), stop=(c == 1))
                last.then_inc(v_ready, 1)

            def turn_negmax(v, h):
                pe.wait_ge(negmax_ready, v * 2 + h + 1)
                nc.tensor.transpose(misc_bf[0:M_ROWS * HG * 4, 0:P], negmax_parts[:, :, :, :].rearrange("p r g q -> p (r g q)"),
                                    eye_b[:, :]).then_inc(negmax_turned, 1)

            def turn_out(v, h):
                pe.wait_ge(acc_copied, v * 2 + h + 1)
                for t in range(4):
                    last = nc.tensor.transpose(misc_ps[:, t * P:(t + 1) * P], acc_sb[:, t * P:(t + 1) * P], eye_f[:, :])
                last.then_inc(out_turned, 1)

            def rowmax_scores(v, par, m, r0, r1, first=False):
                if m == 0 and r0 == 0:
                    pe.wait_ge(k_loaded, (v + 1) * (SLOTS * 16))
                    pe.wait_ge(q_loaded, (v + 1) * (SLOTS * 16))
                for r in range(4 * m + r0, 4 * m + r1):
                    qt, g, kh = r // 8, r % 8 // 2, r % 2
                    if not (first and r < 2):
                        pe.wait_ge(rowmax_read, v * (4 * STEPS) + (r - 1))
                    nc.tensor.matmul(rowmax_ps[kh][:, :], q_st[par][0:ROWS, qt // 4, g, qt % 4 * P:(qt % 4 + 1) * P],
                                     k_st[par][0:ROWS, g, kh * HALF:(kh + 1) * HALF], start=True, stop=True)\
                        .then_inc(rowmax_ready, 1)

            def scores(v, par, s, p, first=False):
                step = v * STEPS + s
                if s % KT == 0 and p == 0:
                    pe.wait_ge(negmax_placed, (v * 2 + (s // KT + 1)) * (M_ROWS * 16))
                if not first:
                    pe.wait_ge(probs_ready, step * 2 + (p - 1))
                for g in range(2):
                    last = nc.tensor.matmul(scores_ps[p][:, g * HALF:(g + 1) * HALF],
                                            k_st[par][:, 2 * p + g, s % KT * P:(s % KT + 1) * P],
                                            q_st[par][:, s // KT, 2 * p + g, :], start=True, stop=True)
                last.then_inc(scores_ready, 1)

            def values(v, par, s, first=False):
                step = v * STEPS + s
                pe.wait_ge(probs_ready, step * 2 + 2)
                if s == 0:
                    pe.wait_ge(v_placed, v + 1)
                if s % KT == 0 and not first:
                    pe.wait_ge(acc_copied, v * 2 + s // KT)
                for g in range(HG):
                    last = nc.tensor.matmul(acc_ps[g * VW:(g + 1) * VW, :], v_sb[par][:, s % KT, g, :],
                                            probs[s % 2][:, g, :], start=(s % KT == 0), stop=(s % KT == KT - 1),
                                            skip_group_check=True)
                last.then_inc(pv_done, 1)

            def unit(u, par, this, next_, after):
                opening = not this
                for s in range(CUT, STEPS + CUT):
                    v, vpar, vs, exists = step_of(u, par, s, this, next_)
                    w, wpar, ws, more = maxima_of(u, par, s, this, next_)
                    at_start = opening and s == STEPS
                    if exists:
                        scores(v, vpar, vs, 0, first=at_start)
                    if more:
                        rowmax_scores(w, wpar, ws, 0, 2, first=opening)
                    if exists:
                        scores(v, vpar, vs, 1, first=at_start)
                        if s == STEPS and this or s > STEPS or s < STEPS and vs > 0:
                            values(*((u, par, STEPS - 1) if s == STEPS else (v, vpar, vs - 1)), first=opening)
                    elif s == STEPS and this:
                        values(u, par, STEPS - 1)
                    if more:
                        rowmax_scores(w, wpar, ws, 2, 4)
                    if s == CUT and after:
                        if this:
                            pe.wait_ge(out_done, u * 2 + 1)
                        else:
                            pe.wait_ge(v_copied, 1)
                        project_qk(u + 2, pair_of(u, par), 0)
                    if s == CUT + 2 and this:
                        if after:
                            pe.wait_ge(raw_copied, u * 2 + 5)
                        else:
                            pe.wait_ge(out_done, u * 2 + 1)
                        turn_negmax(u, 1)
                    if s == CUT + 3 and after:
                        if this:
                            pe.wait_ge(negmax_copied, u * 2 + 2)
                        else:
                            pe.wait_ge(raw_copied, u * 2 + 5)
                        project_qk(u + 2, pair_of(u, par), 1)
                    if s == CUT + 6 and after:
                        pe.wait_ge(raw_copied, u * 2 + 6)
                        project_v(u + 2)
                    if s == 11 and this:
                        if after:
                            pe.wait_ge(v_copied, u + 3)
                        else:
                            pe.wait_ge(negmax_copied, u * 2 + 2)
                        turn_out(u, 0)
                    if s == 13 and next_:
                        if this:
                            pe.wait_ge(out_done, u * 2 + 2)
                        else:
                            pe.wait_ge(v_copied, u + 3)
                        turn_negmax(u + 1, 0)
                    if s == STEPS + 2 and this:
                        if next_:
                            pe.wait_ge(negmax_copied, u * 2 + 3)
                        else:
                            pe.wait_ge(out_done, u * 2 + 2)
                        turn_out(u, 1)
                if opening:
                    pe.wait_ge(negmax_copied, 1)

            def pair_of(u, par):
                return 0 if isinstance(u, int) and u == -1 else (u + 2 - par) // 2

            pe.wait_ge(consts, 3 * 16)
            pe.wait_ge(ones_set, 7)
            project_qk(0, 0, 0)
            pe.wait_ge(raw_copied, 1)
            project_qk(0, 0, 1)
            pe.wait_ge(raw_copied, 2)
            project_v(0)
            units(pe, unit)

        @block.scalar
        def _(act):
            def copy_raw(v, h, first=False):
                act.wait_ge(qk_ready, v * 2 + h + 1)
                if not first:
                    act.wait_ge(roped_done, v * 2 + (h - 1))
                nc.scalar.copy(raw[:, h, :], misc_ps[:, :]).then_inc(raw_copied, 1)

            def copy_v(v, first=False):
                act.wait_ge(v_ready, v + 1)
                if not first:
                    act.wait_ge(v_placed, v)
                nc.scalar.copy(v_raw[:, :, :, :].rearrange("p t g d -> p (t g d)"), misc_ps[:, :]).then_inc(v_copied, 1)

            def part_hi(v, h, first=False):
                act.wait_ge(roped_done, v * 2 + h + 1)
                if not first:
                    act.wait_ge(parts_out[h], v * (2 * PARTS * 16))
                nc.scalar.copy(part[0][:, h, :], roped[:, h, :]).then_inc(hi_done, 1)

            def copy_acc(v, h):
                act.wait_ge(pv_done, v * STEPS + (h + 1) * KT)
                act.wait_ge(out_done, v * 2 + h + 1)
                nc.scalar.copy(acc_sb[:, :], acc_ps[:, :]).then_inc(acc_copied, 1)

            def unit(u, par, this, next_, after):
                for s in range(CUT, STEPS + CUT):
                    v, vpar, vs, exists = step_of(u, par, s, this, next_)
                    if exists:
                        for p in range(2):
                            step = v * STEPS + vs
                            act.wait_ge(scores_ready, step * 2 + (p + 1))
                            if this or vs > 1:
                                act.wait_ge(pv_done, step - 1)
                            nc.scalar.activation(probs[vs % 2][:, 2 * p:2 * p + 2, :].rearrange("p g t -> p (g t)"),
                                                 scores_ps[p][:, :], ACT.Exp, scale=SCALE).then_inc(probs_ready, 1)
                    if s == CUT + 1 and after:
                        copy_raw(u + 2, 0)
                    if s == CUT + 4 and after:
                        copy_raw(u + 2, 1)
                        part_hi(u + 2, 0)
                    if s == 8 and this:
                        copy_acc(u, 0)
                    if s == CUT + 7 and after:
                        copy_v(u + 2)
                        part_hi(u + 2, 1)
                    if s == STEPS and this:
                        copy_acc(u, 1)

            act.wait_ge(ones_set, 7)
            copy_raw(0, 0, first=True)
            copy_raw(0, 1, first=True)
            copy_v(0, first=True)
            part_hi(0, 0, first=True)
            part_hi(0, 1, first=True)
            units(act, unit)

        @block.vector
        def _(dve):
            swap_mask = [lane ^ 1 for lane in range(32)]

            def swap(v, h):
                wait_apart(dve, (consts, 3 * 16), (raw_copied, v * 2 + h + 1))
                nc.vector.stream_shuffle(swapped[:, h, :], raw[:, h, :], swap_mask).then_inc(swap_done, 1)

            def take_maxima(v, m):
                for r in range(4 * m, 4 * m + 4):
                    qt, g, kh = r // 8, r % 8 // 2, r % 2
                    dve.wait_ge(rowmax_ready, v * (4 * STEPS) + (r + 1))
                    nc.vector.tensor_reduce(halfmax[:, qt % 4, g, kh:kh + 1], rowmax_ps[kh][:, :], AX.X, ALU.max,
                                            negate=True).then_inc(rowmax_read, 1)

            def split_maxima(v, h, first=False):
                n = v * 2 + h
                dve.wait_ge(rowmax_read, v * (4 * STEPS) + (h + 1) * (2 * STEPS))
                nc.vector.tensor_tensor(negmax[:, :, :], halfmax[:, :, :, 0].rearrange("p q g -> p g q"),
                                        halfmax[:, :, :, 1].rearrange("p q g -> p g q"), ALU.min).then_inc(negmax_step, 1)
                dve.wait_ge(negmax_step, n * 2 + 1)
                if not first:
                    dve.wait_ge(negmax_turned, n)
                nc.vector.tensor_copy(negmax_parts[:, 0, :, :], negmax[:, :, :]).then_inc(negmax_step, 1)
                dve.wait_ge(negmax_step, n * 2 + 2)
                nc.vector.tensor_tensor(negmax_parts[:, 1, :, :], negmax[:, :, :], negmax_parts[:, 0, :, :],
                                        ALU.subtract).then_inc(negmax_ready, 1)

            def copy_negmax(v, h, first=False):
                n = v * 2 + h
                dve.wait_ge(negmax_turned, n + 1)
                if not first:
                    dve.wait_ge(negmax_placed, n * (M_ROWS * 16))
                nc.vector.tensor_copy(negmax_t[:, :], misc_bf[0:M_ROWS * HG * 4, 0:P]).then_inc(negmax_copied, 1)

            def normalise(v, h):
                n = v * 2 + h
                dve.wait_ge(out_turned, n + 1)
                out4 = misc_ps[:, :].rearrange("p (t g c) -> p t g c", g=HG, c=VW)
                nc.vector.reciprocal(recip[:, :, :], out4[:, :, :, HD]).then_inc(recip_done, 1)
                dve.wait_ge(recip_done, n + 1)
                dst = attn[:, bass.ds(v * (KT * HG * HD) + h * (4 * HG * HD), 4 * HG * HD)]
                nc.vector.tensor_tensor(dst.rearrange("p (t g d) -> p t g d", g=HG, d=HD), out4[:, :, :, 0:HD],
                                        recip[:, :, :].unsqueeze(3).broadcast_to([P, 4, HG, HD]), ALU.mult).then_inc(out_done, 1)

            def unit(u, par, this, next_, after):
                for s in range(CUT, STEPS + CUT):
                    w, wpar, ws, more = maxima_of(u, par, s, this, next_)
                    if more:
                        take_maxima(w, ws)
                    if s == CUT and this:
                        split_maxima(u, 1)
                    if s == CUT + 2 and after:
                        swap(u + 2, 0)
                    if s == CUT + 2 and this:
                        copy_negmax(u, 1)
                    if s == CUT + 5 and after:
                        swap(u + 2, 1)
                    if s == 11 and next_:
                        split_maxima(u + 1, 0, first=not this)
                    if s == 11 and this:
                        normalise(u, 0)
                    if s == 13 and next_:
                        copy_negmax(u + 1, 0, first=not this)
                    if s == STEPS + 2 and this:
                        normalise(u, 1)

            for p in range(2):
                nc.vector.memset(k_st[p][ROWS:ROWS + M_ROWS, :, :], 1.0).then_inc(ones_set, 1)
            nc.vector.memset(recip[:, :, :], 1.0).then_inc(out_done, 1)
            dve.wait_ge(consts, 3 * 16)
            nc.vector.tensor_copy(eye_b[:, :], eye_f[:, :]).then_inc(ones_set, 1)
            swap(0, 0)
            swap(0, 1)
            units(dve, unit)

        @block.gpsimd
        def _(pool):
            def rope(v, h):
                lo, hi = h * HALF, (h + 1) * HALF
                pool.wait_ge(swap_done, v * 2 + h + 1)
                nc.gpsimd.tensor_tensor(term_c[:, :], raw[:, h, :], cos_sb[:, lo:hi], ALU.mult).then_inc(terms_done, 1)
                nc.gpsimd.tensor_tensor(term_s[:, :], swapped[:, h, :], sin_sb[:, lo:hi], ALU.mult).then_inc(terms_done, 1)
                pool.wait_ge(terms_done, v * 4 + 2 * h + 2)
                nc.gpsimd.tensor_tensor(roped[:, h, :], term_c[:, :], term_s[:, :], ALU.add).then_inc(roped_done, 1)

            def split(v, h):
                pool.wait_ge(hi_done, v * 2 + h + 1)
                nc.gpsimd.tensor_tensor(rest[:, :], roped[:, h, :], part[0][:, h, :], ALU.subtract).then_inc(mid_done, 1)
                nc.gpsimd.tensor_tensor(part[1][:, h, :], roped[:, h, :], part[0][:, h, :], ALU.subtract).then_inc(mid_done, 1)
                pool.wait_ge(mid_done, v * 4 + 2 * h + 2)
                nc.gpsimd.tensor_tensor(part[2][:, h, :], rest[:, :], part[1][:, h, :], ALU.subtract).then_inc(lo_done, 1)

            def place_v(v, par, first=False):
                wait_apart(pool, (zeros_set, 1), (v_copied, v + 1), *([] if first else [(pv_done, (v - 1) * STEPS)]))
                nc.gpsimd.tensor_copy(v_sb[par][:, :, :, 0:HD], v_raw[:, :, :, :]).then_inc(v_placed, 1)

            def unit(u, par, this, next_, after):
                if after:
                    rope(u + 2, 0)
                    split(u + 2, 0)
                    rope(u + 2, 1)
                    split(u + 2, 1)
                    place_v(u + 2, par, first=not this)

            for p in range(2):
                nc.gpsimd.memset(v_sb[p][:, :, :, :], 0.0).then_inc(ones_set, 1)
            pool.wait_ge(ones_set, 5)
            for p in range(2):
                nc.gpsimd.memset(v_sb[p][:, :, :, HD:HD + 1], 1.0).then_inc(ones_set, 1)
            nc.gpsimd.memset(zeros[:, :], 0.0).then_inc(zeros_set, 1)
            pool.wait_ge(zeros_set, 1)
            routed_rows = rows_dram[T:, :].rearrange("(n p r) c -> n p (r c)", p=P, r=10)
            for n in range(routed_rows.shape[0]):
                nc.gpsimd.dma_start(routed_rows[n], zeros[:, :]).then_inc(rows_cleared, 16)
            pool.wait_ge(consts, 3 * 16)
            pool.wait_ge(ones_set, 7)
            rope(0, 0)
            split(0, 0)
            rope(0, 1)
            split(0, 1)
            place_v(0, 0, first=True)
            units(pool, unit)
            pool.wait_ge(rows_cleared, routed_rows.shape[0] * 16)


def in_turn(engine, n, slots, lag, emit):
    for j in range(slots):
        emit(j, j, lambda l, j=j: j >= l)
    with engine.Fori(1, n // slots) as i:
        for k in range(slots):
            emit(i * slots + k, k, lambda l: True)
    for j in range(n, n + lag):
        emit(j, j % slots, lambda l, j=j: j - l < n)


QUAD = 4
TILES = T // P
QUADS = TILES // QUAD
W_ROW = 2 * 2 * F + D
ROUTED_TILES = (2 * T) // P + EXPERTS
ALL_TILES = TILES + ROUTED_TILES


def attention_norm_router(nc, x, w_proj, gate_w, eye, attn, rows_dram, router, load_weights):
    with ExitStack() as ctx:
        def sb(name, shape, dt=F32):
            return ctx.enter_context(nc.sbuf_tensor(name, shape, dt))

        def ps(name, shape, dt=F32):
            return ctx.enter_context(nc.psum_tensor(name, shape, dt))

        def sem(name):
            return ctx.enter_context(nc.semaphore(name))

        attn_t_ps = ps("attn_t_ps", [P, QUAD * D])
        proj_ps = ps("proj_ps", [P, QUAD * D])
        x1_t_ps = ps("x1_t_ps", [P, QUAD * D])
        logits_ps = ps("logits_ps", [P, QUAD * EXPERTS])

        ident = sb("ident", [P, P])
        wp_sb = sb("wp_sb", [P, 2, D])
        wg_sb = sb("wg_sb", [P, 2, EXPERTS])
        half_power = sb("half_power", [P, QUAD])
        attn_q = [sb(f"attn_q{p}", [P, QUAD, D]) for p in range(2)]
        x_q = [sb(f"x_q{p}", [P, QUAD, D]) for p in range(2)]
        attn_t = [sb(f"attn_t{p}", [P, QUAD * D]) for p in range(2)]
        summed = sb("summed", [P, QUAD, D])
        stats = sb("stats", [P, QUAD, 6])
        meanvar = sb("meanvar", [P, QUAD, 2])
        var_eps = sb("var_eps", [P, QUAD])
        rstd = sb("rstd", [P, QUAD])
        x1_q = [sb(f"x1_q{p}", [P, QUAD, D]) for p in range(2)]
        x1_t = [sb(f"x1_t{p}", [P, QUAD * D]) for p in range(2)]

        small = sem("small")
        weights = sem("weights")
        power_set = sem("power_set")
        inputs = [sem(f"inputs{p}") for p in range(2)]
        attn_turned = sem("attn_turned")
        attn_copied = sem("attn_copied")
        proj_ready = sem("proj_ready")
        summed_done = sem("summed_done")
        stats_done = sem("stats_done")
        meanvar_done = sem("meanvar_done")
        var_done = sem("var_done")
        rstd_done = sem("rstd_done")
        x1_done = sem("x1_done")
        x1_stored = [sem(f"x1_stored{p}") for p in range(2)]
        x1_turned = sem("x1_turned")
        x1_copied = sem("x1_copied")
        logits_ready = sem("logits_ready")
        router_done = sem("router_done")

        block = ctx.enter_context(nc.Block())

        @block.sync
        def _(sp):
            def quad(g, par, exists):
                if exists(0):
                    if not (isinstance(g, int) and g < 2):
                        sp.wait_ge(attn_turned, g - 1)
                        sp.wait_ge(summed_done, g - 1)
                    b, h = g // 2, g % 2
                    for u in range(GROUPS):
                        at = b * (GROUPS * KT * HG * HD) + u * (KT * HG * HD) + h * (QUAD * HG * HD)
                        sp.dma_start(attn_q[par][:, :, u * HG * HD:(u + 1) * HG * HD],
                                     attn[:, bass.ds(at, QUAD * HG * HD)].rearrange("p (t c) -> p t c", t=QUAD)).then_inc(inputs[par], 16)
                    sp.dma_start(x_q[par][:, :, :], x[bass.ds(g * (QUAD * P), QUAD * P), :].rearrange("(t p) c -> p t c", p=P))\
                        .then_inc(inputs[par], 16)
                if exists(1):
                    sp.wait_ge(x1_done, g)
                    sp.dma_start(rows_dram[bass.ds((g - 1) * (QUAD * P), QUAD * P), :].rearrange("(t p) c -> p t c", p=P),
                                 x1_q[1 - par][:, :, :]).then_inc(x1_stored[1 - par], 16)

            sp.dma_start(ident[:, :], eye).then_inc(small, 16)
            sp.dma_start(wp_sb[:, :, :], w_proj.rearrange("(c p) n -> p c n", p=P)).then_inc(small, 16)
            sp.dma_start(wg_sb[:, :, :], gate_w.rearrange("(c p) n -> p c n", p=P)).then_inc(small, 16)
            in_turn(sp, QUADS, 2, 1, quad)
            for p in range(2):
                sp.wait_ge(x1_stored[p], QUADS // 2 * 16)

        @block.tensor
        def _(pe):
            def quad(g, par, exists):
                if exists(0):
                    pe.wait_ge(inputs[par], (g // 2 + 1) * ((GROUPS + 1) * 16))
                    if not (isinstance(g, int) and g == 0):
                        pe.wait_ge(attn_copied, g)
                    for t in range(QUAD):
                        for c in range(2):
                            last = nc.tensor.transpose(attn_t_ps[:, (2 * t + c) * P:(2 * t + c + 1) * P],
                                                       attn_q[par][:, t, c * P:(c + 1) * P], ident[:, :])
                    last.then_inc(attn_turned, 1)
                if exists(1):
                    pe.wait_ge(x1_done, g)
                    if not (isinstance(g, int) and g < 2):
                        pe.wait_ge(x1_copied, g - 1)
                    for t in range(QUAD):
                        for c in range(2):
                            last = nc.tensor.transpose(x1_t_ps[:, (2 * t + c) * P:(2 * t + c + 1) * P],
                                                       x1_q[1 - par][:, t, c * P:(c + 1) * P], ident[:, :])
                    last.then_inc(x1_turned, 1)
                if exists(0):
                    pe.wait_ge(attn_copied, g + 1)
                    if not (isinstance(g, int) and g == 0):
                        pe.wait_ge(summed_done, g)
                    for t in range(QUAD):
                        for c in range(2):
                            last = nc.tensor.matmul(proj_ps[:, t * D:(t + 1) * D], attn_t[par][:, (2 * t + c) * P:(2 * t + c + 1) * P],
                                                    wp_sb[:, c, :], start=(c == 0), stop=(c == 1))
                    last.then_inc(proj_ready, 1)
                if exists(1):
                    pe.wait_ge(x1_copied, g)
                    if not (isinstance(g, int) and g < 2):
                        pe.wait_ge(router_done, g - 1)
                    for t in range(QUAD):
                        for c in range(2):
                            last = nc.tensor.matmul(logits_ps[:, t * EXPERTS:(t + 1) * EXPERTS],
                                                    x1_t[1 - par][:, (2 * t + c) * P:(2 * t + c + 1) * P],
                                                    wg_sb[:, c, :], start=(c == 0), stop=(c == 1))
                    last.then_inc(logits_ready, 1)

            pe.wait_ge(small, 3 * 16)
            in_turn(pe, QUADS, 2, 1, quad)

        @block.scalar
        def _(act):
            def quad(g, par, exists):
                if exists(0):
                    act.wait_ge(attn_turned, g + 1)
                    if not (isinstance(g, int) and g < 2):
                        act.wait_ge(proj_ready, g - 1)
                    nc.scalar.copy(attn_t[par][:, :], attn_t_ps[:, :]).then_inc(attn_copied, 1)
                if exists(1):
                    act.wait_ge(x1_turned, g)
                    if not (isinstance(g, int) and g < 3):
                        act.wait_ge(logits_ready, g - 2)
                    nc.scalar.copy(x1_t[1 - par][:, :], x1_t_ps[:, :]).then_inc(x1_copied, 1)
                    act.wait_ge(logits_ready, g)
                    nc.scalar.activation(router[:, bass.ds((g - 1) * (QUAD * EXPERTS), QUAD * EXPERTS)], logits_ps[:, :],
                                         ACT.Sigmoid).then_inc(router_done, 1)

            n = load_weights(act, weights)
            in_turn(act, QUADS, 2, 1, quad)
            act.wait_ge(weights, n)

        @block.vector
        def _(dve):
            def quad(g, par, exists):
                dve.wait_ge(proj_ready, g + 1)
                dve.wait_ge(inputs[par], (g // 2 + 1) * ((GROUPS + 1) * 16))
                nc.vector.tensor_tensor(summed[:, :, :].rearrange("p t c -> p (t c)"), proj_ps[:, :],
                                        x_q[par][:, :, :].rearrange("p t c -> p (t c)"), ALU.add).then_inc(summed_done, 1)
                dve.wait_ge(summed_done, g + 1)
                for t in range(QUAD):
                    nc.vector.bn_stats(stats[:, t, :], summed[:, t, :]).then_inc(stats_done, 1)
                for t in range(QUAD):
                    wait_apart(dve, (small, 3 * 16), (stats_done, g * QUAD + (t + 1)))
                    nc.vector.bn_aggr(meanvar[:, t, :], stats[:, t, :]).then_inc(meanvar_done, 1)
                dve.wait_ge(meanvar_done, g * QUAD + QUAD)
                nc.vector.tensor_scalar_add(var_eps[:, :], meanvar[:, :, 1], EPS).then_inc(var_done, 1)
                dve.wait_ge(rstd_done, g + 1)
                if not (isinstance(g, int) and g < 2):
                    dve.wait_ge(x1_stored[par], g // 2 * 16)
                    dve.wait_ge(x1_turned, g - 1)
                for t in range(QUAD):
                    last = nc.vector.tensor_scalar(x1_q[par][:, t, :], summed[:, t, :], meanvar[:, t, 0:1], rstd[:, t:t + 1],
                                                   ALU.subtract, ALU.mult)
                last.then_inc(x1_done, 1)

            in_turn(dve, QUADS, 2, 0, quad)

        @block.gpsimd
        def _(pool):
            def quad(g, par, exists):
                pool.wait_ge(var_done, g + 1)
                nc.gpsimd.tensor_tensor(rstd[:, :], var_eps[:, :], half_power[:, :], ALU.pow).then_inc(rstd_done, 1)

            nc.gpsimd.memset(half_power[:, :], -0.5).then_inc(power_set, 1)
            pool.wait_ge(power_set, 1)
            in_turn(pool, QUADS, 2, 0, quad)


def route(nc, router, bias, before, iota_dram, gains, slots, tile_weights):
    with ExitStack() as ctx:
        def sb(name, shape, dt=F32):
            return ctx.enter_context(nc.sbuf_tensor(name, shape, dt))

        def sem(name):
            return ctx.enter_context(nc.semaphore(name))

        N = TILES * EXPERTS
        rank_ps = ctx.enter_context(nc.psum_tensor("rank_ps", [P, N], F32))
        total_ps = ctx.enter_context(nc.psum_tensor("total_ps", [P, N], F32))
        bias_sb = sb("bias_sb", [P, EXPERTS])
        before_sb = sb("before_sb", [P, P])
        before_b = sb("before_b", [P, P], BF16)
        ones_b = sb("ones_b", [P, P], BF16)
        falling = sb("falling", [P, EXPERTS])
        restart = sb("restart", [P, EXPERTS, TILES])
        tile_no = sb("tile_no", [P, ROUTED_TILES])
        biased = sb("biased", [P, TILES, EXPERTS])
        best = sb("best", [P, TILES])
        marks = sb("marks", [P, TILES, EXPERTS])
        chosen = sb("chosen", [P, 2, TILES, EXPERTS])
        product = sb("product", [P, 2, TILES, EXPERTS])
        score = sb("score", [P, 2, TILES])
        score_sum = sb("score_sum", [P, TILES])
        both_b = sb("both_b", [P, TILES, EXPERTS], BF16)
        total = sb("total", [P, EXPERTS, TILES])
        running = sb("running", [P, EXPERTS, TILES])
        count_i = sb("count_i", [P, EXPERTS], I32)
        tiles_of = sb("tiles_of", [P, EXPERTS])
        ends = sb("ends", [P, EXPERTS])
        starts = sb("starts", [P, EXPERTS])
        ones_e = sb("ones_e", [P, EXPERTS])
        place = sb("place", [P, TILES, EXPERTS])
        ended = sb("ended", [P, ROUTED_TILES, EXPERTS])
        expert_of = sb("expert_of", [P, ROUTED_TILES])

        loaded = sem("loaded")
        step = sem("step")
        sel_ready = sem("sel_ready")
        counted = sem("counted")

        block = ctx.enter_context(nc.Block())

        @block.sync
        def _(sp):
            sp.dma_start(bias_sb[:, :], bias).then_inc(loaded, 16)
            sp.dma_start(before_sb[:, :], before).then_inc(loaded, 16)
            sp.dma_start(falling[:, :], iota_dram[:, 0:EXPERTS]).then_inc(loaded, 16)
            sp.dma_start(restart[:, :, :].rearrange("p e t -> p (e t)"), iota_dram[:, EXPERTS:EXPERTS + N]).then_inc(loaded, 16)
            sp.dma_start(tile_no[:, :], iota_dram[:, EXPERTS + N:EXPERTS + N + ROUTED_TILES]).then_inc(loaded, 16)

        @block.tensor
        def _(pe):
            pe.wait_ge(sel_ready, 3)
            nc.tensor.matmul(rank_ps[:, :], before_b[:, :], both_b[:, :, :].rearrange("p t e -> p (t e)"),
                             start=True, stop=True).then_inc(counted, 1)
            nc.tensor.matmul(total_ps[:, :], ones_b[:, :], both_b[:, :, :].rearrange("p t e -> p (t e)"),
                             start=True, stop=True).then_inc(counted, 1)

        @block.vector
        def _(dve):
            v = nc.vector
            done = [0]

            def then(instruction):
                done[0] += 1
                instruction.then_inc(step, 1)
                dve.wait_ge(step, done[0])

            def wide(ap):
                return ap.unsqueeze(2).broadcast_to([P, TILES, EXPERTS])

            def per_tile(ap, n=TILES):
                return ap.unsqueeze(1).broadcast_to([P, n, EXPERTS])

            scores3 = router[:, :].rearrange("p (t e) -> p t e", e=EXPERTS)
            dve.wait_ge(loaded, 5 * 16)
            v.tensor_copy(before_b[:, :], before_sb[:, :]).then_inc(sel_ready, 1)
            v.memset(ones_b[:, :], 1.0).then_inc(sel_ready, 1)
            then(v.memset(ones_e[:, :], 1.0))
            then(v.tensor_tensor(biased[:, :, :], scores3, per_tile(bias_sb[:, :]), ALU.add))
            for k in range(2):
                then(v.tensor_reduce(best[:, :], biased[:, :, :], AX.X, ALU.max))
                then(v.tensor_tensor(marks[:, :, :], biased[:, :, :], wide(best[:, :]), ALU.is_equal))
                then(v.tensor_tensor(marks[:, :, :], marks[:, :, :], per_tile(falling[:, :]), ALU.mult))
                then(v.tensor_reduce(best[:, :], marks[:, :, :], AX.X, ALU.max))
                then(v.tensor_tensor(chosen[:, k, :, :], per_tile(falling[:, :]), wide(best[:, :]), ALU.is_equal))
                if k == 0:
                    then(v.scalar_tensor_tensor(biased[:, :, :], chosen[:, 0, :, :], -3.0e38, biased[:, :, :], ALU.mult, ALU.add))
            v.tensor_tensor(both_b[:, :, :], chosen[:, 0, :, :], chosen[:, 1, :, :], ALU.add).then_inc(sel_ready, 1)
            for k in range(2):
                then(v.tensor_tensor(product[:, k, :, :], chosen[:, k, :, :], scores3, ALU.mult))
            then(v.tensor_reduce(score[:, :, :], product[:, :, :, :], AX.X, ALU.add))
            then(v.tensor_tensor(score_sum[:, :], score[:, 0, :], score[:, 1, :], ALU.add))
            then(v.tensor_scalar_add(score_sum[:, :], score_sum[:, :], 1e-20))
            then(v.reciprocal(score_sum[:, :], score_sum[:, :]))
            for k in range(2):
                then(v.tensor_tensor(gains[:, k * TILES:(k + 1) * TILES], score[:, k, :], score_sum[:, :], ALU.mult))
            dve.wait_ge(counted, 2)
            then(v.tensor_copy(total[:, :, :], total_ps[:, :].rearrange("p (t e) -> p e t", e=EXPERTS)))
            flat = "p e t -> p (e t)"
            then(v.tensor_tensor_scan(running[:, :, :].rearrange(flat), restart[:, :, :].rearrange(flat),
                                      total[:, :, :].rearrange(flat), 0.0, ALU.mult, ALU.add))
            then(v.tensor_scalar_add(tiles_of[:, :], running[:, :, TILES - 1], float(P - 1)))
            then(v.tensor_copy(count_i[:, :], tiles_of[:, :]))
            then(v.tensor_scalar(count_i[:, :], count_i[:, :], 7, None, ALU.arith_shift_right))
            then(v.tensor_copy(tiles_of[:, :], count_i[:, :]))
            then(v.tensor_tensor_scan(ends[:, :], ones_e[:, :], tiles_of[:, :], 0.0, ALU.mult, ALU.add))
            then(v.tensor_tensor(starts[:, :], ends[:, :], tiles_of[:, :], ALU.subtract))
            then(v.tensor_scalar(starts[:, :], starts[:, :], float(P), float(T), ALU.mult, ALU.add))
            then(v.tensor_tensor(running[:, :, :], running[:, :, :], total[:, :, :], ALU.subtract))
            then(v.tensor_tensor(place[:, :, :], rank_ps[:, :].rearrange("p (t e) -> p t e", e=EXPERTS),
                                 running[:, :, :].rearrange("p e t -> p t e"), ALU.add))
            then(v.tensor_tensor(place[:, :, :], place[:, :, :], per_tile(starts[:, :]), ALU.add))
            for k in range(2):
                then(v.tensor_tensor(product[:, k, :, :], chosen[:, k, :, :], place[:, :, :], ALU.mult))
            then(v.tensor_reduce(score[:, :, :], product[:, :, :, :], AX.X, ALU.add))
            then(v.tensor_copy(slots[:, :], score[:, :, :].rearrange("p k t -> p (k t)")))
            then(v.tensor_tensor(ended[:, :, :], per_tile(ends[:, :], ROUTED_TILES),
                                 tile_no[:, :].unsqueeze(2).broadcast_to([P, ROUTED_TILES, EXPERTS]), ALU.is_le))
            then(v.tensor_reduce(expert_of[:, :], ended[:, :, :], AX.X, ALU.add))
            then(v.tensor_scalar(expert_of[:, :], expert_of[:, :], float(EXPERTS - 1), float(W_ROW), ALU.min, ALU.mult))
            then(v.memset(tile_weights[:, 0:TILES], EXPERTS * W_ROW))
            then(v.tensor_copy(tile_weights[:, TILES:ALL_TILES], expert_of[0:1, :]))


def experts(nc, eye, weights, slots, tile_weights, rows_dram, out_dram):
    SLOT = 8
    N_QUADS = ALL_TILES // QUAD
    with ExitStack() as ctx:
        def sb(name, shape, dt=F32):
            return ctx.enter_context(nc.sbuf_tensor(name, shape, dt))

        def ps(name, shape, dt=F32):
            return ctx.enter_context(nc.psum_tensor(name, shape, dt))

        def sem(name):
            return ctx.enter_context(nc.semaphore(name))

        rows_t_ps = [ps(f"rows_t_ps{p}", [P, 512]) for p in range(2)]
        gate_up_ps = [ps(f"gate_up_ps{p}", [P, 512]) for p in range(2)]
        hidden_t_ps = [ps(f"hidden_t_ps{p}", [P, 512]) for p in range(2)]
        down_ps = [ps(f"down_ps{p}", [P, 512]) for p in range(2)]
        idn = sb("idn", [P, P])
        rows = [sb(f"rows{q}", [P, QUAD, D]) for q in range(2)]
        rows_t = [sb(f"rows_t{p}", [P, D]) for p in range(2)]
        gate = [sb(f"gate{p}", [P, F]) for p in range(2)]
        hidden = [sb(f"hidden{p}", [P, F]) for p in range(2)]
        hidden_t = [sb(f"hidden_t{p}", [P, P]) for p in range(2)]
        result = [sb(f"result{q}", [P, QUAD, D]) for q in range(2)]
        to_scatter = [sb(f"to_scatter{q}", [P, QUAD, D]) for q in range(2)]
        slot_q = [sb(f"slot_q{q}", [P, 2, QUAD], U32) for q in range(2)]

        idn_loaded = sem("idn_loaded")
        rows_loaded = [sem(f"rows_loaded{q}") for q in range(2)]
        scatter_loaded = [sem(f"scatter_loaded{q}") for q in range(2)]
        slots_staged = sem("slots_staged")
        scattered = [sem(f"scattered{q}") for q in range(2)]
        rows_turned = sem("rows_turned")
        rows_copied = sem("rows_copied")
        gate_up_done = sem("gate_up_done")
        gate_done = sem("gate_done")
        hidden_done = sem("hidden_done")
        hidden_turned = sem("hidden_turned")
        hidden_copied = sem("hidden_copied")
        down_done = sem("down_done")
        result_copied = sem("result_copied")
        stored = [sem(f"stored{q}") for q in range(2)]

        block = ctx.enter_context(nc.Block())

        def static_below(j, n):
            return isinstance(j, int) and j < n

        @block.sync
        def _(sp):
            def load(q, par):
                if not static_below(q, 2):
                    sp.wait_ge(rows_turned, (q - 1) * QUAD)
                sp.dma_start(rows[par][:, :, :], rows_dram[bass.ds(q * (QUAD * P), QUAD * P), :].rearrange("(t p) c -> p t c", p=P))\
                    .then_inc(rows_loaded[par], 16)

            def store(q, par):
                sp.wait_ge(result_copied, (q + 1) * QUAD)
                sp.dma_start(out_dram[bass.ds(q * (QUAD * P), QUAD * P), :].rearrange("(t p) c -> p t c", p=P),
                             result[par][:, :, :]).then_inc(stored[par], 16)

            def load_for_scatter(q, par):
                if not static_below(q, 2):
                    sp.wait_ge(scattered[par], (q // 2) * (2 * QUAD * 16))
                sp.dma_start(to_scatter[par][:, :, :], rows_dram[bass.ds(q * (QUAD * P), QUAD * P), :].rearrange("(t p) c -> p t c", p=P))\
                    .then_inc(scatter_loaded[par], 16)

            sp.dma_start(idn[:, :], eye).then_inc(idn_loaded, 16)
            for q in range(2):
                load(q, q)
                load_for_scatter(q, q)
            with sp.Fori(1, QUADS // 2) as i:
                for par in range(2):
                    load(i * 2 + par, par)
                    load_for_scatter(i * 2 + par, par)
                    store(i * 2 + (par - 2), par)
            for par in range(2):
                sp.wait_ge(scattered[par], QUADS // 2 * (2 * QUAD * 16))
            with sp.Fori(QUADS // 2, N_QUADS // 2) as i:
                for par in range(2):
                    load(i * 2 + par, par)
                    store(i * 2 + (par - 2), par)
            for par in range(2):
                store(N_QUADS - 2 + par, par)
            for par in range(2):
                sp.wait_ge(stored[par], N_QUADS // 2 * 16)

        @block.gpsimd
        def _(pool):
            def scatter(q, par, exists):
                if not static_below(q, 2):
                    wait_apart(pool, (idn_loaded, 16), (scattered[par], (q // 2) * (2 * QUAD * 16)))
                for k in range(2):
                    nc.gpsimd.tensor_copy(slot_q[par][:, k, :], slots[:, bass.ds(q * QUAD + k * TILES, QUAD)]).then_inc(slots_staged, 1)
                wait_apart(pool, (idn_loaded, 16), (slots_staged, q * 2 + 2), (scatter_loaded[par], (q // 2 + 1) * 16))
                for t in range(QUAD):
                    for k in range(2):
                        nc.gpsimd.indirect_dma_start(rows_dram, bass.IndirectOffsetOnAxis(slot_q[par][:, k, t:t + 1], 0),
                                                     to_scatter[par][:, t, :], None).then_inc(scattered[par], 16)

            in_turn(pool, QUADS, 2, 0, scatter)
            for par in range(2):
                pool.wait_ge(scattered[par], QUADS // 2 * (2 * QUAD * 16))

        @block.tensor
        def _(pe):
            def tile(j, k, exists):
                if exists(0):
                    q = k // QUAD
                    if k % QUAD == 0:
                        pe.wait_ge(rows_loaded[q], (j // SLOT + 1) * 16)
                    if not static_below(j, 2):
                        pe.wait_ge(rows_copied, j - 1)
                    for c in range(2):
                        last = nc.tensor.transpose(rows_t_ps[k % 2][:, c * P:(c + 1) * P], rows[q][:, k % QUAD, c * P:(c + 1) * P], idn[:, :])
                    last.then_inc(rows_turned, 1)
                if exists(1):
                    n = (k - 1) % 2
                    at = pe.value_load(tile_weights[0:1, bass.ds(j - 1, 1)], min_val=0, max_val=EXPERTS * W_ROW)
                    pe.wait_ge(rows_copied, j)
                    if not static_below(j, 3):
                        pe.wait_ge(hidden_done, j - 2)
                    for c in range(2):
                        last = nc.tensor.matmul(gate_up_ps[n][:, 0:2 * F], rows_t[n][:, c * P:(c + 1) * P],
                                                weights[:, bass.ds(at + c * 2 * F, 2 * F)], start=(c == 0), stop=(c == 1))
                    last.then_inc(gate_up_done, 1)
                if exists(2):
                    n = k % 2
                    pe.wait_ge(hidden_done, j - 1)
                    if not static_below(j, 4):
                        pe.wait_ge(hidden_copied, j - 3)
                    nc.tensor.transpose(hidden_t_ps[n][:, 0:P], hidden[n][:, :], idn[:, :]).then_inc(hidden_turned, 1)
                if exists(3):
                    n = (k - 1) % 2
                    at = pe.value_load(tile_weights[0:1, bass.ds(j - 3, 1)], min_val=0, max_val=EXPERTS * W_ROW)
                    pe.wait_ge(hidden_copied, j - 2)
                    if not static_below(j, 5):
                        pe.wait_ge(result_copied, j - 4)
                    nc.tensor.matmul(down_ps[n][:, 0:D], hidden_t[n][:, :], weights[:, bass.ds(at + 4 * F, D)],
                                     start=True, stop=True).then_inc(down_done, 1)

            pe.wait_ge(idn_loaded, 16)
            in_turn(pe, ALL_TILES, SLOT, 3, tile)

        @block.scalar
        def _(act):
            def tile(j, k, exists):
                if exists(1):
                    n = (k - 1) % 2
                    act.wait_ge(gate_up_done, j)
                    if not static_below(j, 3):
                        act.wait_ge(hidden_done, j - 2)
                    nc.scalar.activation(gate[n][:, :], gate_up_ps[n][:, 0:F], ACT.Silu).then_inc(gate_done, 1)
                if exists(3):
                    n, r = (k - 1) % 2, (k - 3) % SLOT
                    act.wait_ge(down_done, j - 2)
                    if r % QUAD == 0 and not static_below(j, SLOT + 3):
                        act.wait_ge(stored[r // QUAD], (j - 3) // SLOT * 16)
                    nc.scalar.copy(result[r // QUAD][:, r % QUAD, :], down_ps[n][:, 0:D]).then_inc(result_copied, 1)

            in_turn(act, ALL_TILES, SLOT, 3, tile)

        @block.vector
        def _(dve):
            def tile(j, k, exists):
                if exists(0):
                    dve.wait_ge(rows_turned, j + 1)
                    if not static_below(j, 2):
                        dve.wait_ge(gate_up_done, j - 1)
                    nc.vector.tensor_copy(rows_t[k % 2][:, :], rows_t_ps[k % 2][:, 0:D]).then_inc(rows_copied, 1)
                if exists(1):
                    n = (k - 1) % 2
                    dve.wait_ge(gate_done, j)
                    if not static_below(j, 3):
                        dve.wait_ge(hidden_turned, j - 2)
                    nc.vector.tensor_tensor(hidden[n][:, :], gate_up_ps[n][:, F:2 * F], gate[n][:, :], ALU.mult).then_inc(hidden_done, 1)
                if exists(2):
                    n = k % 2
                    dve.wait_ge(hidden_turned, j - 1)
                    if not static_below(j, 4):
                        dve.wait_ge(down_done, j - 3)
                    nc.vector.tensor_copy(hidden_t[n][:, :], hidden_t_ps[n][:, 0:P]).then_inc(hidden_copied, 1)

            in_turn(dve, ALL_TILES, SLOT, 2, tile)


def combine(nc, slots, gains, rows_dram, out_dram, out):
    with ExitStack() as ctx:
        def sb(name, shape, dt=F32):
            return ctx.enter_context(nc.sbuf_tensor(name, shape, dt))

        def sem(name):
            return ctx.enter_context(nc.semaphore(name))

        minus_half = sb("minus_half", [P, QUAD])
        slot_g = [sb(f"slot_g{q}", [P, 2, QUAD], U32) for q in range(2)]
        routed = [sb(f"routed{q}", [P, 2, QUAD, D]) for q in range(2)]
        x1_g = [sb(f"x1_g{q}", [P, QUAD, D]) for q in range(2)]
        shared_g = [sb(f"shared_g{q}", [P, QUAD, D]) for q in range(2)]
        total_g = [sb(f"total_g{q}", [P, QUAD, D]) for q in range(2)]
        stats_g = sb("stats_g", [P, QUAD, 6])
        meanvar_g = [sb(f"meanvar_g{q}", [P, QUAD, 2]) for q in range(2)]
        var_g = sb("var_g", [P, QUAD])
        rstd_g = sb("rstd_g", [P, QUAD])
        shift_g = sb("shift_g", [P, QUAD])
        normed = [sb(f"normed{q}", [P, QUAD, D]) for q in range(2)]

        half_set = sem("half_set")
        staged_g = sem("staged_g")
        gathered = [sem(f"gathered{q}") for q in range(2)]
        fetched = [sem(f"fetched{q}") for q in range(2)]
        first_added = sem("first_added")
        second_added = sem("second_added")
        shared_added = sem("shared_added")
        stats_g_done = sem("stats_g_done")
        meanvar_g_done = sem("meanvar_g_done")
        var_g_done = sem("var_g_done")
        rstd_g_done = sem("rstd_g_done")
        shift_done = sem("shift_done")
        normed_done = sem("normed_done")
        out_stored = [sem(f"out_stored{q}") for q in range(2)]

        block = ctx.enter_context(nc.Block())

        def static_below(j, n):
            return isinstance(j, int) and j < n

        def rows_of(dram, q):
            return dram[bass.ds(q * (QUAD * P), QUAD * P), :].rearrange("(t p) c -> p t c", p=P)

        @block.sync
        def _(sp):
            def quad(q, par, exists):
                if exists(0):
                    if not static_below(q, 2):
                        sp.wait_ge(shared_added, q - 1)
                    sp.dma_start(x1_g[par][:, :, :], rows_of(rows_dram, q)).then_inc(fetched[par], 16)
                    sp.dma_start(shared_g[par][:, :, :], rows_of(out_dram, q)).then_inc(fetched[par], 16)
                if exists(1):
                    sp.wait_ge(normed_done, q)
                    sp.dma_start(rows_of(out, q - 1), normed[1 - par][:, :, :]).then_inc(out_stored[1 - par], 16)

            in_turn(sp, QUADS, 2, 1, quad)
            for par in range(2):
                sp.wait_ge(out_stored[par], QUADS // 2 * 16)

        @block.gpsimd
        def _(pool):
            def quad(q, par, exists):
                if exists(0):
                    if not static_below(q, 2):
                        wait_apart(pool, (half_set, 1), (gathered[par], q // 2 * (2 * QUAD * 16)), (second_added, (q - 1) * QUAD))
                    for k in range(2):
                        nc.gpsimd.tensor_copy(slot_g[par][:, k, :], slots[:, bass.ds(q * QUAD + k * TILES, QUAD)]).then_inc(staged_g, 1)
                    wait_apart(pool, (half_set, 1), (staged_g, q * 2 + 2))
                    for t in range(QUAD):
                        for k in range(2):
                            nc.gpsimd.indirect_dma_start(routed[par][:, k, t, :], None, out_dram,
                                                         bass.IndirectOffsetOnAxis(slot_g[par][:, k, t:t + 1], 0))\
                                .then_inc(gathered[par], 16)
                if exists(1):
                    pool.wait_ge(var_g_done, q)
                    if not static_below(q, 2):
                        pool.wait_ge(normed_done, q - 1)
                    nc.gpsimd.tensor_tensor(rstd_g[:, :], var_g[:, :], minus_half[:, :], ALU.pow).then_inc(rstd_g_done, 1)

            nc.gpsimd.memset(minus_half[:, :], -0.5).then_inc(half_set, 1)
            pool.wait_ge(half_set, 1)
            in_turn(pool, QUADS, 2, 1, quad)

        @block.vector
        def _(dve):
            def quad(q, par, exists):
                if exists(0):
                    dve.wait_ge(fetched[par], (q // 2 + 1) * 32)
                    dve.wait_ge(gathered[par], (q // 2 + 1) * (2 * QUAD * 16))
                    if not static_below(q, 2):
                        dve.wait_ge(normed_done, q - 1)
                    for t in range(QUAD):
                        nc.vector.scalar_tensor_tensor(total_g[par][:, t, :], routed[par][:, 0, t, :], gains[:, bass.ds(q * QUAD + t, 1)],
                                                       x1_g[par][:, t, :], ALU.mult, ALU.add).then_inc(first_added, 1)
                    for t in range(QUAD):
                        dve.wait_ge(first_added, q * QUAD + (t + 1))
                        nc.vector.scalar_tensor_tensor(total_g[par][:, t, :], routed[par][:, 1, t, :],
                                                       gains[:, bass.ds(q * QUAD + (TILES + t), 1)],
                                                       total_g[par][:, t, :], ALU.mult, ALU.add).then_inc(second_added, 1)
                    dve.wait_ge(second_added, q * QUAD + QUAD)
                    nc.vector.tensor_tensor(total_g[par][:, :, :], total_g[par][:, :, :], shared_g[par][:, :, :], ALU.add)\
                        .then_inc(shared_added, 1)
                    dve.wait_ge(shared_added, q + 1)
                    for t in range(QUAD):
                        nc.vector.bn_stats(stats_g[:, t, :], total_g[par][:, t, :]).then_inc(stats_g_done, 1)
                if exists(1):
                    dve.wait_ge(rstd_g_done, q)
                    if not static_below(q, 2):
                        dve.wait_ge(normed_done, q - 1)
                    nc.vector.scalar_tensor_tensor(shift_g[:, :], meanvar_g[1 - par][:, :, 0], -1.0, rstd_g[:, :],
                                                   ALU.mult, ALU.mult).then_inc(shift_done, 1)
                if exists(0):
                    for t in range(QUAD):
                        wait_apart(dve, (half_set, 1), (stats_g_done, q * QUAD + (t + 1)))
                        nc.vector.bn_aggr(meanvar_g[par][:, t, :], stats_g[:, t, :]).then_inc(meanvar_g_done, 1)
                    dve.wait_ge(meanvar_g_done, q * QUAD + QUAD)
                    nc.vector.tensor_scalar_add(var_g[:, :], meanvar_g[par][:, :, 1], EPS).then_inc(var_g_done, 1)

            in_turn(dve, QUADS, 2, 1, quad)

        @block.scalar
        def _(act):
            def quad(q, par, exists):
                act.wait_ge(shift_done, q + 1)
                if not static_below(q, 2):
                    act.wait_ge(out_stored[par], q // 2 * 16)
                for t in range(QUAD):
                    last = nc.scalar.activation(normed[par][:, t, :], total_g[par][:, t, :], ACT.Identity,
                                                bias=shift_g[:, t:t + 1], scale=rstd_g[:, t:t + 1])
                last.then_inc(normed_done, 1)

            in_turn(act, QUADS, 2, 0, quad)


def transformer_block(nc, x, x_t, w_units, w_proj, gate_w, bias, shared_gate, shared_up, shared_down, gate_up, down,
                      cos_t, sin_t, eye, before, integers, out):
    parts_dram = nc.dram_tensor("parts_dram", (UNITS, 2, PARTS, HD, 2, HG, HALF), BF16, kind="Internal").ap()
    rows_dram = nc.dram_tensor("rows_dram", (ALL_TILES * P, D), F32, kind="Internal").ap()
    out_dram = nc.dram_tensor("out_dram", (ALL_TILES * P, D), F32, kind="Internal").ap()

    with ExitStack() as ctx:
        def sb(name, shape, dt=F32):
            return ctx.enter_context(nc.sbuf_tensor(name, shape, dt))

        router = sb("router", [P, TILES * EXPERTS])
        gains = sb("gains", [P, 2 * TILES])
        slots = sb("slots", [P, 2 * TILES], U32)
        tile_weights = sb("tile_weights", [1, ALL_TILES], I32)
        weights = sb("weights", [P, (EXPERTS + 1) * W_ROW])
        with nc.sbuf_tensor("attn", [P, UNITS * KT * HG * HD], F32) as attn:
            attention(nc, x_t, w_units, cos_t, sin_t, eye, parts_dram, attn, rows_dram)

            def load_weights(engine, signal):
                w3 = weights[:, :].rearrange("p (e n) -> p e n", n=W_ROW)
                for c in range(2):
                    engine.dma_start(w3[:, 0:EXPERTS, c * 2 * F:(c + 1) * 2 * F],
                                     gate_up[:, c * P:(c + 1) * P, :].rearrange("e p n -> p e n")).then_inc(signal, 16)
                    engine.dma_start(w3[:, EXPERTS, c * 2 * F:c * 2 * F + F], shared_gate[c * P:(c + 1) * P, :]).then_inc(signal, 16)
                    engine.dma_start(w3[:, EXPERTS, c * 2 * F + F:(c + 1) * 2 * F], shared_up[c * P:(c + 1) * P, :]).then_inc(signal, 16)
                engine.dma_start(w3[:, 0:EXPERTS, 4 * F:4 * F + D], down.rearrange("e p n -> p e n")).then_inc(signal, 16)
                engine.dma_start(w3[:, EXPERTS, 4 * F:4 * F + D], shared_down).then_inc(signal, 16)
                return 8 * 16

            attention_norm_router(nc, x, w_proj, gate_w, eye, attn, rows_dram, router, load_weights)
        route(nc, router, bias, before, integers, gains, slots, tile_weights)
        experts(nc, eye, weights, slots, tile_weights, rows_dram, out_dram)
        combine(nc, slots, gains, rows_dram, out_dram, out)


def _constants():
    import numpy as np

    freqs = np.float32(1.0) / np.float32(10000.0) ** (np.arange(0, HD, 2, dtype=np.float32) / np.float32(HD))
    angles = np.outer(np.arange(L, dtype=np.float32), freqs).astype(np.float32)
    cos = np.repeat(np.cos(angles), 2, axis=-1).T
    sin = np.repeat(np.sin(angles), 2, axis=-1).T.copy()
    sin[0::2] *= -1
    falling = np.arange(EXPERTS, 0, -1, dtype=np.float32)
    restart = np.tile((np.arange(TILES) > 0).astype(np.float32), EXPERTS)
    tile_no = np.arange(ROUTED_TILES, dtype=np.float32)
    integers = np.concatenate([falling, restart, tile_no])
    return {
        "cos_t": np.tile(cos, (2 * HG, 1)).astype(np.float32),
        "sin_t": np.tile(sin, (2 * HG, 1)).astype(np.float32),
        "eye": np.eye(P, dtype=np.float32),
        "before": np.triu(np.ones((P, P), np.float32), 1),
        "integers": np.ascontiguousarray(np.broadcast_to(integers, (P, integers.size))),
    }


def kernel(**inputs):
    import concourse.bacc as bacc
    import numpy as np
    from concourse.bass_utils import run_bass_kernel_spmd

    a = {name: np.asarray(value) for name, value in inputs.items()}
    x = a["L0_attn_x"]
    arrays = {
        "x": x.reshape(T, D),
        "x_t": x.transpose(0, 2, 1),
        "w_units": a["L0_attn_w_qkv"].reshape(D, 3, GROUPS, HG * HD).transpose(2, 0, 1, 3).reshape(GROUPS, D, 3 * HG * HD),
        "w_proj": a["L0_attn_w_proj"],
        "gate_w": a["L0_ffn_gate_w"],
        "bias": np.broadcast_to(a["L0_ffn_expert_bias"], (P, EXPERTS)),
        "shared_gate": a["L0_ffn_shared_gate_w"],
        "shared_up": a["L0_ffn_shared_up_w"],
        "shared_down": a["L0_ffn_shared_down_w"],
        "gate_up": a["L0_ffn_experts_gate_up"],
        "down": a["L0_ffn_experts_down"],
        **_constants(),
    }
    arrays = {name: np.ascontiguousarray(value) for name, value in arrays.items()}
    nc = bacc.Bacc("TRN2", target_bir_lowering=False, num_devices=1)
    args = {name: nc.dram_tensor(f"in_{name}", value.shape, mybir.dt.from_np(value.dtype), kind="ExternalInput").ap()
            for name, value in arrays.items()}
    out = nc.dram_tensor("out_0", (T, D), F32, kind="ExternalOutput").ap()
    transformer_block(nc, **args, out=out)
    result = run_bass_kernel_spmd(nc, [{f"in_{name}": value for name, value in arrays.items()}], core_ids=[0])
    return result.results[0]["out_0"].reshape(B, L, D)
```

```python
import math
from contextlib import ExitStack

import concourse.bass as bass
from concourse import mybir

P = 128
B, L, D, HEADS, HD = 4, 1024, 256, 16, 16
T = B * L
EXPERTS, F = 16, 128
EPS = 1e-5

HG = 4
GROUPS = HEADS // HG
UNITS = B * GROUPS
KT = L // P
HALF = 512
STEPS = KT * (L // HALF)
BANKS = 3
EXP_COUNT = 2
LEAD = 12
CUT = STEPS - LEAD - 1
PARTS = 3
SLOTS = 6
Q_SLOT = [0, 0, 1, 0, 1, 2]
K_SLOT = [0, 1, 0, 2, 1, 0]
ROWS = SLOTS * HD
M_ROWS = 2
VW = 32
SCALE = 1.0 / math.sqrt(HD)
QUAD = 4
TILES = T // P
QUADS = TILES // QUAD
W_ROW = 2 * 2 * F + D
ROUTED_TILES = (2 * T) // P + EXPERTS
ALL_TILES = TILES + ROUTED_TILES
ROW = D + 1
BLANK = 5

ALU = mybir.AluOpType
ACT = mybir.ActivationFunctionType
AX = mybir.AxisListType
F32 = mybir.dt.float32
BF16 = mybir.dt.bfloat16
I32 = mybir.dt.int32
U32 = mybir.dt.uint32


def wait_apart(engine, constant, *waits):
    waits = [(semaphore, value if isinstance(value, int) else engine.to_reg(value)) for semaphore, value in waits]
    engine.wait_ge(*constant)
    for semaphore, value in waits:
        engine.wait_ge(semaphore, value)


def attention(nc, x_t, w_units, cos_t, sin_t, eye, parts_dram, attn, rows_dram, spare_ids):
    with ExitStack() as ctx:
        def sb(name, shape, dt=F32):
            return ctx.enter_context(nc.sbuf_tensor(name, shape, dt))

        def ps(name, shape, dt=F32):
            return ctx.enter_context(nc.psum_tensor(name, shape, dt))

        def sem(name):
            return ctx.enter_context(nc.semaphore(name))

        scores_ps = [ps(f"scores_ps{n}", [P, HALF]) for n in range(BANKS)]
        rowmax_ps = [ps(f"rowmax_ps{n}", [P, HALF]) for n in range(BANKS)]
        acc_ps = ps("acc_ps", [P, HALF])
        misc_ps = ps("misc_ps", [P, HALF])
        misc_bf = misc_ps[:, :].bitcast(BF16)

        eye_f = sb("eye_f", [P, P])
        eye_b = sb("eye_b", [P, P], BF16)
        cos_sb = sb("cos_sb", [P, L])
        sin_sb = sb("sin_sb", [P, L])
        xt_sb = sb("xt_sb", [P, 2, L])
        w_sb = sb("w_sb", [P, 2, 3 * HG * HD])
        raw = sb("raw", [P, 2, HALF])
        swapped = sb("swapped", [P, 2, HALF])
        term_c = sb("term_c", [P, HALF])
        term_s = sb("term_s", [P, HALF])
        second_c = sb("second_c", [P, HALF])
        second_s = sb("second_s", [P, HALF])
        roped = sb("roped", [P, 2, HALF])
        rest = sb("rest", [P, HALF])
        part = [sb(f"part{n}", [P, 2, HALF], BF16) for n in range(PARTS)]
        v_raw = sb("v_raw", [P, KT, HG, HD])
        v_sb = [sb(f"v_sb{p}", [P, KT, HG, VW]) for p in range(2)]
        q_st = [sb(f"q_st{p}", [ROWS + M_ROWS, 2, HG, HALF], BF16) for p in range(2)]
        k_st = [sb(f"k_st{p}", [ROWS + M_ROWS, HG, L], BF16) for p in range(2)]
        probs = [sb(f"probs{p}", [P, HG, HALF]) for p in range(2)]
        halfmax = sb("halfmax", [P, 4, HG, 2])
        negmax = sb("negmax", [P, HG, 4])
        negmax_parts = sb("negmax_parts", [P, M_ROWS, HG, 4], BF16)
        negmax_t = sb("negmax_t", [M_ROWS * HG * 4, P], BF16)
        acc_sb = sb("acc_sb", [P, HALF])
        recip = sb("recip", [P, 4, HG])
        ids = sb("ids", [P, ROUTED_TILES], U32)
        blank = [sb(f"blank{p}", [P, BLANK, ROW]) for p in range(2)]

        zeros_set = sem("zeros_set")
        ids_loaded = sem("ids_loaded")
        ids_placed = sem("ids_placed")
        rows_cleared = [sem(f"rows_cleared{p}") for p in range(2)]
        consts = sem("consts")
        ones_set = sem("ones_set")
        v_cleared = sem("v_cleared")
        w_loaded = sem("w_loaded")
        x_loaded = sem("x_loaded")
        qk_ready = sem("qk_ready")
        raw_copied = sem("raw_copied")
        v_ready = sem("v_ready")
        v_copied = sem("v_copied")
        v_placed = sem("v_placed")
        swap_done = sem("swap_done")
        terms_done = sem("terms_done")
        roped_done = sem("roped_done")
        hi_done = sem("hi_done")
        mid_done = sem("mid_done")
        lo_done = sem("lo_done")
        second_step = sem("second_step")
        second_roped = sem("second_roped")
        second_hi = sem("second_hi")
        second_lo = sem("second_lo")
        parts_out = [sem(f"parts_out{h}") for h in range(2)]
        k_loaded = sem("k_loaded")
        q_loaded = sem("q_loaded")
        rowmax_ready = sem("rowmax_ready")
        rowmax_read = sem("rowmax_read")
        negmax_step = sem("negmax_step")
        negmax_ready = sem("negmax_ready")
        negmax_turned = sem("negmax_turned")
        negmax_copied = sem("negmax_copied")
        negmax_placed = sem("negmax_placed")
        scores_ready = sem("scores_ready")
        probs_ready = sem("probs_ready")
        pv_done = sem("pv_done")
        acc_copied = sem("acc_copied")
        out_turned = sem("out_turned")
        recip_done = sem("recip_done")
        out_done = sem("out_done")

        block = ctx.enter_context(nc.Block())

        def units(engine, emit):
            emit(-1, 1, False, True, True)
            with engine.Fori(0, UNITS // 2 - 1) as pair:
                emit(pair * 2, 0, True, True, True)
                emit(pair * 2 + 1, 1, True, True, True)
            emit(UNITS - 2, 0, True, True, False)
            emit(UNITS - 1, 1, True, False, False)

        def step_of(u, par, s, this, next_):
            return (u, par, s, this) if s < STEPS else (u + 1, 1 - par, s - STEPS, next_)

        def maxima_of(u, par, s, this, next_):
            if s + LEAD < 2 * STEPS and s + LEAD - STEPS < 0:
                return (u, par, s + LEAD, this)
            m = s + LEAD - STEPS
            return (u, par, m, this) if m < 0 else (u + 1, 1 - par, m, next_) if m < STEPS else (u + 2, par, m - STEPS, False)

        def pool_halves(v, h, each=1):
            return each * (h + 1) if isinstance(v, int) and v == 0 else v * (2 * each) + h * each

        @block.sync
        def _(sp):
            def load_w(v):
                sp.dma_start(w_sb[:, :, :], w_units[v % GROUPS].rearrange("(c p) n -> p c n", p=P)).then_inc(w_loaded, 16)

            def load_x(batch):
                sp.dma_start(xt_sb[:, :, :], x_t[batch].rearrange("(c p) t -> p c t", p=P)).then_inc(x_loaded, 16)

            def write_parts(v, h):
                sp.wait_ge(lo_done, pool_halves(v, h))
                write_half(v, h)

            def write_half(v, h):
                for n in range(PARTS):
                    sp.dma_start(parts_dram[v, 0, n, :, h].rearrange("d h t -> h d t"),
                                 part[n][0:HG * HD, h, :]).then_inc(parts_out[h], 16)
                    sp.dma_start(parts_dram[v, 1, n].rearrange("d a h t -> d (a h t)").rearrange("d (h a t) -> h d a t", a=2, t=HALF)[:, :, h],
                                 part[n][HG * HD:2 * HG * HD, h, :]).then_inc(parts_out[h], 16)

            def load_stacks(v, par):
                for h in range(2):
                    sp.wait_ge(parts_out[h], (v + 1) * (2 * PARTS * 16))
                for slot in range(SLOTS):
                    sp.dma_start(k_st[par][slot * HD:(slot + 1) * HD, :, :].rearrange("d h t -> d (h t)"),
                                 parts_dram[v, 1, K_SLOT[slot]].rearrange("d a h t -> d (a h t)")).then_inc(k_loaded, 16)
                for slot in range(SLOTS):
                    sp.dma_start(q_st[par][slot * HD:(slot + 1) * HD, :, :, :].rearrange("d a h t -> d (a h t)"),
                                 parts_dram[v, 0, Q_SLOT[slot]].rearrange("d a h t -> d (a h t)")).then_inc(q_loaded, 16)

            def place_negmax(v, par, h):
                sp.wait_ge(negmax_copied, v * 2 + h + 1)
                for r in range(M_ROWS):
                    sp.dma_start(q_st[par][ROWS + r:ROWS + r + 1, h, :, :].rearrange("o g (q t) -> o (g q) t", t=P),
                                 negmax_t[r * HG * 4:(r + 1) * HG * 4, :]).then_inc(negmax_placed, 16)

            def unit(u, par, this, next_, after):
                if this:
                    place_negmax(u, par, 1)
                if after:
                    write_parts(u + 2, 0)
                    write_parts(u + 2, 1)
                    sp.wait_ge(v_ready, u + 3)
                    load_w(u + 3)
                    if par:
                        load_x((u + 3) // GROUPS % B)
                if next_:
                    place_negmax(u + 1, 1 - par, 0)
                if after:
                    if this:
                        wait_apart(sp, (consts, 3 * 16), (scores_ready, (u + 1) * (HG * STEPS)))
                    load_stacks(u + 2, par)

            sp.dma_start(eye_f[:, :], eye).then_inc(consts, 16)
            load_w(0)
            load_x(0)
            sp.dma_start(cos_sb[:, :], cos_t).then_inc(consts, 16)
            sp.dma_start(sin_sb[:, :], sin_t).then_inc(consts, 16)
            sp.dma_start(ids[:, :], spare_ids).then_inc(ids_loaded, 16)
            sp.wait_ge(v_ready, 1)
            load_w(1)
            sp.wait_ge(second_lo, 1)
            write_half(0, 1)
            write_parts(0, 0)
            load_stacks(0, 0)
            units(sp, unit)
            sp.wait_ge(w_loaded, (UNITS + 1) * 16)
            sp.wait_ge(x_loaded, (UNITS // 2 + 1) * 16)

        @block.tensor
        def _(pe):
            def project_qk(v, pair, h):
                pe.wait_ge(w_loaded, (v + 1) * 16)
                pe.wait_ge(x_loaded, (pair + 1) * 16)
                for c in range(2):
                    last = nc.tensor.matmul(misc_ps[:, :], w_sb[:, c, 0:2 * HG * HD], xt_sb[:, c, h * HALF:(h + 1) * HALF],
                                            start=(c == 0), stop=(c == 1))
                last.then_inc(qk_ready, 1)

            def project_v(v):
                for t in range(KT):
                    for c in range(2):
                        last = nc.tensor.matmul(misc_ps[:, t * HG * HD:(t + 1) * HG * HD], xt_sb[:, c, t * P:(t + 1) * P],
                                                w_sb[:, c, 2 * HG * HD:3 * HG * HD], start=(c == 0), stop=(c == 1))
                last.then_inc(v_ready, 1)

            def turn_negmax(v, h):
                pe.wait_ge(negmax_ready, v * 2 + h + 1)
                nc.tensor.transpose(misc_bf[0:M_ROWS * HG * 4, 0:P], negmax_parts[:, :, :, :].rearrange("p r g q -> p (r g q)"),
                                    eye_b[:, :]).then_inc(negmax_turned, 1)

            def turn_out(v, h):
                pe.wait_ge(acc_copied, v * 2 + h + 1)
                for t in range(4):
                    last = nc.tensor.transpose(misc_ps[:, t * P:(t + 1) * P], acc_sb[:, t * P:(t + 1) * P], eye_f[:, :])
                last.then_inc(out_turned, 1)

            def rowmax_scores(v, par, m, n, first=False):
                if m == 0 and n == 0:
                    pe.wait_ge(k_loaded, (v + 1) * (SLOTS * 16))
                    pe.wait_ge(q_loaded, (v + 1) * (SLOTS * 16))
                r = 4 * m + n
                qt, g, kh = r // 8, r % 8 // 2, r % 2
                if not (first and r < BANKS):
                    pe.wait_ge(rowmax_read, v * (4 * STEPS) + max(0, r - (BANKS - 1)))
                nc.tensor.matmul(rowmax_ps[r % BANKS][:, :], q_st[par][0:ROWS, qt // 4, g, qt % 4 * P:(qt % 4 + 1) * P],
                                 k_st[par][0:ROWS, g, kh * HALF:(kh + 1) * HALF], start=True, stop=True)\
                    .then_inc(rowmax_ready, 1)

            def scores(v, par, s, g, first=False):
                if s % KT == 0 and g == 0:
                    pe.wait_ge(negmax_placed, (v * 2 + (s // KT + 1)) * (M_ROWS * 16))
                i = s * HG + g
                if not (first and i < BANKS):
                    pe.wait_ge(probs_ready, v * (HG * STEPS * EXP_COUNT) + max(0, i - (BANKS - 1)) * EXP_COUNT)
                nc.tensor.matmul(scores_ps[i % BANKS][:, :], k_st[par][:, g, s % KT * P:(s % KT + 1) * P],
                                 q_st[par][:, s // KT, g, :], start=True, stop=True).then_inc(scores_ready, 1)

            def values(v, par, s, first=False):
                step = v * STEPS + s
                pe.wait_ge(probs_ready, v * (STEPS * HG * EXP_COUNT) + (s * HG + HG) * EXP_COUNT)
                if s == 0:
                    pe.wait_ge(v_placed, v + 1)
                if s % KT == 0 and not first:
                    pe.wait_ge(acc_copied, v * 2 + s // KT)
                for g in range(HG):
                    last = nc.tensor.matmul(acc_ps[g * VW:(g + 1) * VW, :], v_sb[par][:, s % KT, g, :],
                                            probs[s % 2][:, g, :], start=(s % KT == 0), stop=(s % KT == KT - 1),
                                            skip_group_check=True)
                last.then_inc(pv_done, 1)

            def unit(u, par, this, next_, after):
                opening = not this
                if opening:
                    pe.wait_ge(v_copied, 1)
                    project_qk(1, 0, 0)
                    pe.wait_ge(raw_copied, 3)
                    project_qk(1, 0, 1)
                    pe.wait_ge(raw_copied, 4)
                    project_v(1)
                    pe.wait_ge(consts, 3 * 16)
                    pe.wait_ge(ones_set, 3)
                for s in range(CUT, STEPS + CUT):
                    v, vpar, vs, exists = step_of(u, par, s, this, next_)
                    w, wpar, ws, more = maxima_of(u, par, s, this, next_)
                    at_start = opening and s == STEPS
                    for g in range(HG):
                        if exists:
                            scores(v, vpar, vs, g, first=at_start)
                        if more:
                            rowmax_scores(w, wpar, ws, g, first=opening)
                    if this and s == STEPS:
                        values(u, par, STEPS - 1)
                    elif exists and vs > 0:
                        values(v, vpar, vs - 1, first=opening)
                    if s == CUT and this and after:
                        pe.wait_ge(out_done, u * 2 + 1)
                        project_qk(u + 2, pair_of(u, par), 0)
                    if s == CUT + 2 and this:
                        if after:
                            pe.wait_ge(raw_copied, u * 2 + 5)
                        else:
                            pe.wait_ge(out_done, u * 2 + 1)
                        turn_negmax(u, 1)
                    if s == CUT + 3 and this and after:
                        pe.wait_ge(negmax_copied, u * 2 + 2)
                        project_qk(u + 2, pair_of(u, par), 1)
                    if s == CUT + 6 and this and after:
                        pe.wait_ge(raw_copied, u * 2 + 6)
                        project_v(u + 2)
                    if s == 11 and this:
                        if after:
                            pe.wait_ge(v_copied, u + 3)
                        else:
                            pe.wait_ge(negmax_copied, u * 2 + 2)
                        turn_out(u, 0)
                    if s == 13 and next_:
                        if this:
                            pe.wait_ge(out_done, u * 2 + 2)
                        else:
                            pe.wait_ge(v_copied, u + 3)
                        turn_negmax(u + 1, 0)
                    if s == STEPS + 2 and this:
                        if next_:
                            pe.wait_ge(negmax_copied, u * 2 + 3)
                        else:
                            pe.wait_ge(out_done, u * 2 + 2)
                        turn_out(u, 1)
                if opening:
                    pe.wait_ge(negmax_copied, 1)

            def pair_of(u, par):
                return (u + 2 - par) // 2

            project_qk(0, 0, 0)
            pe.wait_ge(raw_copied, 1)
            project_qk(0, 0, 1)
            pe.wait_ge(raw_copied, 2)
            project_v(0)
            units(pe, unit)

        @block.scalar
        def _(act):
            def copy_raw(v, h, first=False):
                act.wait_ge(qk_ready, v * 2 + h + 1)
                if not first:
                    act.wait_ge(roped_done, 1 if isinstance(v, int) and v == 1 else v * 2 + (h - 2))
                nc.scalar.copy(raw[:, h, :], misc_ps[:, :]).then_inc(raw_copied, 1)

            def copy_v(v, first=False):
                act.wait_ge(v_ready, v + 1)
                if not first:
                    act.wait_ge(v_placed, v)
                nc.scalar.copy(v_raw[:, :, :, :].rearrange("p t g d -> p (t g d)"), misc_ps[:, :]).then_inc(v_copied, 1)

            def part_hi(v, h, first=False):
                act.wait_ge(roped_done, pool_halves(v, h))
                if not first:
                    act.wait_ge(parts_out[h], v * (2 * PARTS * 16))
                nc.scalar.copy(part[0][:, h, :], roped[:, h, :]).then_inc(hi_done, 1)

            def copy_acc(v, h):
                act.wait_ge(pv_done, v * STEPS + (h + 1) * KT)
                act.wait_ge(out_done, v * 2 + h + 1)
                nc.scalar.copy(acc_sb[:, :], acc_ps[:, :]).then_inc(acc_copied, 1)

            def unit(u, par, this, next_, after):
                if not this:
                    copy_raw(1, 0)
                    copy_raw(1, 1)
                    copy_v(1)
                    part_hi(1, 0)
                    part_hi(1, 1)
                for s in range(CUT, STEPS + CUT):
                    v, vpar, vs, exists = step_of(u, par, s, this, next_)
                    if exists:
                        step = v * STEPS + vs
                        for g in range(HG):
                            act.wait_ge(scores_ready, step * HG + (g + 1))
                            if g == 0 and (this or vs > 1):
                                act.wait_ge(pv_done, step - 1)
                            nc.scalar.activation(probs[vs % 2][:, g, :], scores_ps[(vs * HG + g) % BANKS][:, :], ACT.Exp,
                                                 scale=SCALE).then_inc(probs_ready, EXP_COUNT)
                    if s == CUT + 1 and this and after:
                        copy_raw(u + 2, 0)
                    if s == CUT + 4 and this and after:
                        copy_raw(u + 2, 1)
                        part_hi(u + 2, 0)
                    if s == 8 and this:
                        copy_acc(u, 0)
                    if s == CUT + 7 and this and after:
                        copy_v(u + 2)
                        part_hi(u + 2, 1)
                    if s == STEPS and this:
                        copy_acc(u, 1)

            copy_raw(0, 0, first=True)
            copy_raw(0, 1, first=True)
            copy_v(0, first=True)
            act.wait_ge(second_roped, 1)
            nc.scalar.copy(part[0][:, 1, :], roped[:, 1, :]).then_inc(second_hi, 1)
            part_hi(0, 0, first=True)
            units(act, unit)

        @block.vector
        def _(dve):
            swap_mask = [lane ^ 1 for lane in range(32)]

            def swap(v, h):
                wait_apart(dve, (consts, 3 * 16), (raw_copied, v * 2 + h + 1))
                nc.vector.stream_shuffle(swapped[:, h, :], raw[:, h, :], swap_mask).then_inc(swap_done, 1)

            def take_maxima(v, m):
                for r in range(4 * m, 4 * m + 4):
                    qt, g, kh = r // 8, r % 8 // 2, r % 2
                    dve.wait_ge(rowmax_ready, v * (4 * STEPS) + (r + 1))
                    nc.vector.tensor_reduce(halfmax[:, qt % 4, g, kh:kh + 1], rowmax_ps[r % BANKS][:, :], AX.X, ALU.max,
                                            negate=True).then_inc(rowmax_read, 1)

            def split_maxima(v, h, first=False):
                n = v * 2 + h
                dve.wait_ge(rowmax_read, v * (4 * STEPS) + (h + 1) * (2 * STEPS))
                nc.vector.tensor_tensor(negmax[:, :, :], halfmax[:, :, :, 0].rearrange("p q g -> p g q"),
                                        halfmax[:, :, :, 1].rearrange("p q g -> p g q"), ALU.min).then_inc(negmax_step, 1)
                dve.wait_ge(negmax_step, n * 2 + 1)
                if not first:
                    dve.wait_ge(negmax_turned, n)
                nc.vector.tensor_copy(negmax_parts[:, 0, :, :], negmax[:, :, :]).then_inc(negmax_step, 1)
                dve.wait_ge(negmax_step, n * 2 + 2)
                nc.vector.tensor_tensor(negmax_parts[:, 1, :, :], negmax[:, :, :], negmax_parts[:, 0, :, :],
                                        ALU.subtract).then_inc(negmax_ready, 1)

            def copy_negmax(v, h, first=False):
                n = v * 2 + h
                dve.wait_ge(negmax_turned, n + 1)
                if not first:
                    dve.wait_ge(negmax_placed, n * (M_ROWS * 16))
                nc.vector.tensor_copy(negmax_t[:, :], misc_bf[0:M_ROWS * HG * 4, 0:P]).then_inc(negmax_copied, 1)

            def normalise(v, h):
                n = v * 2 + h
                dve.wait_ge(out_turned, n + 1)
                out4 = misc_ps[:, :].rearrange("p (t g c) -> p t g c", g=HG, c=VW)
                nc.vector.reciprocal(recip[:, :, :], out4[:, :, :, HD]).then_inc(recip_done, 1)
                dve.wait_ge(recip_done, n + 1)
                dst = attn[:, bass.ds(v * (KT * HG * HD) + h * (4 * HG * HD), 4 * HG * HD)]
                nc.vector.tensor_tensor(dst.rearrange("p (t g d) -> p t g d", g=HG, d=HD), out4[:, :, :, 0:HD],
                                        recip[:, :, :].unsqueeze(3).broadcast_to([P, 4, HG, HD]), ALU.mult).then_inc(out_done, 1)

            def unit(u, par, this, next_, after):
                if not this:
                    swap(1, 0)
                    swap(1, 1)
                for s in range(CUT, STEPS + CUT):
                    w, wpar, ws, more = maxima_of(u, par, s, this, next_)
                    if more:
                        take_maxima(w, ws)
                    if s == CUT and this:
                        split_maxima(u, 1)
                    if s == CUT + 2 and this and after:
                        swap(u + 2, 0)
                    if s == CUT + 2 and this:
                        copy_negmax(u, 1)
                    if s == CUT + 5 and this and after:
                        swap(u + 2, 1)
                    if s == 11 and next_:
                        split_maxima(u + 1, 0, first=not this)
                    if s == 11 and this:
                        normalise(u, 0)
                    if s == 13 and next_:
                        copy_negmax(u + 1, 0, first=not this)
                    if s == STEPS + 2 and this:
                        normalise(u, 1)

            nc.vector.memset(recip[:, :, :], 1.0).then_inc(out_done, 1)
            nc.vector.memset(k_st[0][ROWS:ROWS + M_ROWS, :, :], 1.0).then_inc(ones_set, 1)
            dve.wait_ge(consts, 3 * 16)
            nc.vector.tensor_copy(eye_b[:, :], eye_f[:, :]).then_inc(ones_set, 1)
            swap(0, 0)
            swap(0, 1)
            nc.vector.tensor_tensor(second_c[:, :], raw[:, 1, :], cos_sb[:, HALF:], ALU.mult).then_inc(second_step, 1)
            dve.wait_ge(swap_done, 2)
            nc.vector.tensor_tensor(second_s[:, :], swapped[:, 1, :], sin_sb[:, HALF:], ALU.mult).then_inc(second_step, 1)
            dve.wait_ge(second_step, 2)
            nc.vector.tensor_tensor(roped[:, 1, :], second_c[:, :], second_s[:, :], ALU.add).then_inc(second_roped, 1)
            dve.wait_ge(second_hi, 1)
            nc.vector.tensor_tensor(second_c[:, :], roped[:, 1, :], part[0][:, 1, :], ALU.subtract).then_inc(second_step, 1)
            nc.vector.tensor_tensor(part[1][:, 1, :], roped[:, 1, :], part[0][:, 1, :], ALU.subtract).then_inc(second_step, 1)
            dve.wait_ge(second_step, 4)
            nc.vector.tensor_tensor(part[2][:, 1, :], second_c[:, :], part[1][:, 1, :], ALU.subtract).then_inc(second_lo, 1)
            nc.vector.memset(k_st[1][ROWS:ROWS + M_ROWS, :, :], 1.0).then_inc(ones_set, 1)
            units(dve, unit)

        @block.gpsimd
        def _(pool):
            def rope(v, h):
                lo, hi = h * HALF, (h + 1) * HALF
                pool.wait_ge(swap_done, v * 2 + h + 1)
                nc.gpsimd.tensor_tensor(term_c[:, :], raw[:, h, :], cos_sb[:, lo:hi], ALU.mult).then_inc(terms_done, 1)
                nc.gpsimd.tensor_tensor(term_s[:, :], swapped[:, h, :], sin_sb[:, lo:hi], ALU.mult).then_inc(terms_done, 1)
                pool.wait_ge(terms_done, pool_halves(v, h, 2))
                nc.gpsimd.tensor_tensor(roped[:, h, :], term_c[:, :], term_s[:, :], ALU.add).then_inc(roped_done, 1)

            def split(v, h):
                pool.wait_ge(hi_done, pool_halves(v, h))
                nc.gpsimd.tensor_tensor(rest[:, :], roped[:, h, :], part[0][:, h, :], ALU.subtract).then_inc(mid_done, 1)
                nc.gpsimd.tensor_tensor(part[1][:, h, :], roped[:, h, :], part[0][:, h, :], ALU.subtract).then_inc(mid_done, 1)
                pool.wait_ge(mid_done, pool_halves(v, h, 2))
                nc.gpsimd.tensor_tensor(part[2][:, h, :], rest[:, :], part[1][:, h, :], ALU.subtract).then_inc(lo_done, 1)

            def place_v(v, par, first=False):
                wait_apart(pool, (zeros_set, 1), (v_copied, v + 1), *([] if first else [(pv_done, (v - 1) * STEPS)]))
                nc.gpsimd.tensor_copy(v_sb[par][:, :, :, 0:HD], v_raw[:, :, :, :]).then_inc(v_placed, 1)

            def unit(u, par, this, next_, after):
                if after:
                    rope(u + 2, 0)
                    split(u + 2, 0)
                    rope(u + 2, 1)
                    split(u + 2, 1)
                    place_v(u + 2, par, first=not this)

            for p in range(2):
                nc.gpsimd.memset(v_sb[p][:, :, :, :], 0.0).then_inc(v_cleared, 1)
            pool.wait_ge(v_cleared, 2)
            for p in range(2):
                nc.gpsimd.memset(v_sb[p][:, :, :, HD:HD + 1], 1.0).then_inc(v_cleared, 1)
            for p in range(2):
                nc.gpsimd.memset(blank[p][:, :, :], 0.0).then_inc(zeros_set, 1)
            pool.wait_ge(consts, 3 * 16)
            pool.wait_ge(v_cleared, 4)
            rope(0, 0)
            split(0, 0)
            place_v(0, 0, first=True)
            units(pool, unit)
            routed_rows = rows_dram[T:, :].rearrange("(n p r) c -> n p (r c)", p=P, r=BLANK)
            pool.wait_ge(ids_loaded, 16)
            pool.wait_ge(zeros_set, 2)
            for n in range(ROUTED_TILES // BLANK):
                if n >= 2:
                    pool.wait_ge(rows_cleared[n % 2], n // 2 * 16)
                nc.gpsimd.tensor_copy(blank[n % 2][:, :, :].bitcast(U32)[:, :, D], ids[:, n * BLANK:(n + 1) * BLANK]).then_inc(ids_placed, 1)
                pool.wait_ge(ids_placed, n + 1)
                nc.gpsimd.dma_start(routed_rows[n], blank[n % 2][:, :, :].rearrange("p r c -> p (r c)")).then_inc(rows_cleared[n % 2], 16)
            for p in range(2):
                pool.wait_ge(rows_cleared[p], ROUTED_TILES // BLANK // 2 * 16)


def in_turn(engine, n, slots, lag, emit, before=1):
    before = max(before, -(-lag // slots))
    for j in range(before * slots):
        emit(j, j % slots, lambda l, j=j: j >= l)
    with engine.Fori(before, n // slots) as i:
        for k in range(slots):
            emit(i * slots + k, k, lambda l: True)
    for j in range(n, n + lag):
        emit(j, j % slots, lambda l, j=j: j - l < n)


def attention_norm_router(nc, x, w_proj, gate_w, eye, attn, rows_dram, router):
    with ExitStack() as ctx:
        def sb(name, shape, dt=F32):
            return ctx.enter_context(nc.sbuf_tensor(name, shape, dt))

        def ps(name, shape, dt=F32):
            return ctx.enter_context(nc.psum_tensor(name, shape, dt))

        def sem(name):
            return ctx.enter_context(nc.semaphore(name))

        attn_t_ps = ps("attn_t_ps", [P, QUAD * D])
        proj_ps = ps("proj_ps", [P, QUAD * D])
        x1_t_ps = ps("x1_t_ps", [P, QUAD * D])
        logits_ps = ps("logits_ps", [P, QUAD * EXPERTS])

        ident = sb("ident", [P, P])
        wp_sb = sb("wp_sb", [P, 2, D])
        wg_sb = sb("wg_sb", [P, 2, EXPERTS])
        half_power = sb("half_power", [P, QUAD])
        attn_q = [sb(f"attn_q{p}", [P, QUAD, D]) for p in range(2)]
        x_q = [sb(f"x_q{p}", [P, QUAD, D]) for p in range(2)]
        attn_t = [sb(f"attn_t{p}", [P, QUAD * D]) for p in range(2)]
        summed = sb("summed", [P, QUAD, D])
        stats = sb("stats", [P, QUAD, 6])
        meanvar = sb("meanvar", [P, QUAD, 2])
        var_eps = sb("var_eps", [P, QUAD])
        rstd = sb("rstd", [P, QUAD])
        x1_q = [sb(f"x1_q{p}", [P, QUAD, D]) for p in range(2)]
        x1_t = [sb(f"x1_t{p}", [P, QUAD * D]) for p in range(2)]

        small = sem("small")
        power_set = sem("power_set")
        inputs = [sem(f"inputs{p}") for p in range(2)]
        attn_sorted = sem("attn_sorted")
        attn_turned = sem("attn_turned")
        attn_copied = sem("attn_copied")
        proj_ready = sem("proj_ready")
        summed_done = sem("summed_done")
        stats_done = sem("stats_done")
        meanvar_done = sem("meanvar_done")
        var_done = sem("var_done")
        rstd_done = sem("rstd_done")
        x1_done = sem("x1_done")
        x1_stored = [sem(f"x1_stored{p}") for p in range(2)]
        x1_turned = sem("x1_turned")
        x1_copied = sem("x1_copied")
        logits_ready = sem("logits_ready")
        router_done = sem("router_done")

        block = ctx.enter_context(nc.Block())

        @block.sync
        def _(sp):
            def quad(g, par, exists):
                if exists(0):
                    if not (isinstance(g, int) and g < 2):
                        sp.wait_ge(summed_done, g - 1)
                    sp.dma_start(x_q[par][:, :, :], x[bass.ds(g * (QUAD * P), QUAD * P), :].rearrange("(t p) c -> p t c", p=P))\
                        .then_inc(inputs[par], 16)
                if exists(1):
                    sp.wait_ge(x1_done, g)
                    sp.dma_start(rows_dram[bass.ds((g - 1) * (QUAD * P), QUAD * P), 0:D].rearrange("(t p) c -> p t c", p=P),
                                 x1_q[1 - par][:, :, :]).then_inc(x1_stored[1 - par], 16)

            sp.dma_start(ident[:, :], eye).then_inc(small, 16)
            sp.dma_start(wp_sb[:, :, :], w_proj.rearrange("(c p) n -> p c n", p=P)).then_inc(small, 16)
            sp.dma_start(wg_sb[:, :, :], gate_w.rearrange("(c p) n -> p c n", p=P)).then_inc(small, 16)
            in_turn(sp, QUADS, 2, 1, quad)
            for p in range(2):
                sp.wait_ge(x1_stored[p], QUADS // 2 * 16)

        @block.tensor
        def _(pe):
            def quad(g, par, exists):
                def static_below(n):
                    return isinstance(g, int) and g < n

                if exists(1):
                    pe.wait_ge(attn_copied, g)
                    if not static_below(2):
                        pe.wait_ge(summed_done, g - 1)
                    for t in range(QUAD):
                        for c in range(2):
                            last = nc.tensor.matmul(proj_ps[:, t * D:(t + 1) * D], attn_t[1 - par][:, (2 * t + c) * P:(2 * t + c + 1) * P],
                                                    wp_sb[:, c, :], start=(c == 0), stop=(c == 1))
                    last.then_inc(proj_ready, 1)
                if exists(0):
                    pe.wait_ge(attn_sorted, g + 1)
                    if not static_below(1):
                        pe.wait_ge(attn_copied, g)
                    for t in range(QUAD):
                        for c in range(2):
                            last = nc.tensor.transpose(attn_t_ps[:, (2 * t + c) * P:(2 * t + c + 1) * P],
                                                       attn_q[par][:, t, c * P:(c + 1) * P], ident[:, :])
                    last.then_inc(attn_turned, 1)
                if exists(2):
                    pe.wait_ge(x1_done, g - 1)
                    if not static_below(3):
                        pe.wait_ge(x1_copied, g - 2)
                    for t in range(QUAD):
                        for c in range(2):
                            last = nc.tensor.transpose(x1_t_ps[:, (2 * t + c) * P:(2 * t + c + 1) * P],
                                                       x1_q[par][:, t, c * P:(c + 1) * P], ident[:, :])
                    last.then_inc(x1_turned, 1)
                if exists(3):
                    pe.wait_ge(x1_copied, g - 2)
                    if not static_below(4):
                        pe.wait_ge(router_done, g - 3)
                    for t in range(QUAD):
                        for c in range(2):
                            last = nc.tensor.matmul(logits_ps[:, t * EXPERTS:(t + 1) * EXPERTS],
                                                    x1_t[1 - par][:, (2 * t + c) * P:(2 * t + c + 1) * P],
                                                    wg_sb[:, c, :], start=(c == 0), stop=(c == 1))
                    last.then_inc(logits_ready, 1)

            pe.wait_ge(small, 3 * 16)
            in_turn(pe, QUADS, 2, 3, quad)

        @block.scalar
        def _(act):
            def quad(g, par, exists):
                if exists(0):
                    act.wait_ge(attn_turned, g + 1)
                    if not (isinstance(g, int) and g < 2):
                        act.wait_ge(proj_ready, g - 1)
                    nc.scalar.copy(attn_t[par][:, :], attn_t_ps[:, :]).then_inc(attn_copied, 1)
                if exists(2):
                    act.wait_ge(x1_turned, g - 1)
                    if not (isinstance(g, int) and g < 4):
                        act.wait_ge(logits_ready, g - 3)
                    nc.scalar.copy(x1_t[par][:, :], x1_t_ps[:, :]).then_inc(x1_copied, 1)
                if exists(3):
                    act.wait_ge(logits_ready, g - 2)
                    nc.scalar.activation(router[:, bass.ds((g - 3) * (QUAD * EXPERTS), QUAD * EXPERTS)], logits_ps[:, :],
                                         ACT.Sigmoid).then_inc(router_done, 1)

            in_turn(act, QUADS, 2, 3, quad)

        @block.vector
        def _(dve):
            def quad(g, par, exists):
                dve.wait_ge(proj_ready, g + 1)
                if not (isinstance(g, int) and g == 0):
                    dve.wait_ge(x1_done, g)
                dve.wait_ge(inputs[par], (g // 2 + 1) * 16)
                nc.vector.tensor_tensor(summed[:, :, :].rearrange("p t c -> p (t c)"), proj_ps[:, :],
                                        x_q[par][:, :, :].rearrange("p t c -> p (t c)"), ALU.add).then_inc(summed_done, 1)
                dve.wait_ge(summed_done, g + 1)
                for t in range(QUAD):
                    nc.vector.bn_stats(stats[:, t, :], summed[:, t, :]).then_inc(stats_done, 1)
                for t in range(QUAD):
                    wait_apart(dve, (small, 3 * 16), (stats_done, g * QUAD + (t + 1)))
                    nc.vector.bn_aggr(meanvar[:, t, :], stats[:, t, :]).then_inc(meanvar_done, 1)
                dve.wait_ge(meanvar_done, g * QUAD + QUAD)
                nc.vector.tensor_scalar_add(var_eps[:, :], meanvar[:, :, 1], EPS).then_inc(var_done, 1)
                dve.wait_ge(rstd_done, g + 1)
                if not (isinstance(g, int) and g < 2):
                    dve.wait_ge(x1_stored[par], g // 2 * 16)
                    dve.wait_ge(x1_turned, g - 1)
                for t in range(QUAD):
                    last = nc.vector.tensor_scalar(x1_q[par][:, t, :], summed[:, t, :], meanvar[:, t, 0:1], rstd[:, t:t + 1],
                                                   ALU.subtract, ALU.mult)
                last.then_inc(x1_done, 1)

            in_turn(dve, QUADS, 2, 0, quad)

        @block.gpsimd
        def _(pool):
            def quad(g, par, exists):
                if exists(0):
                    if not (isinstance(g, int) and g < 2):
                        wait_apart(pool, (power_set, 1), (attn_turned, g - 1))
                    batch = attn[:, bass.ds(g // 2 * (GROUPS * KT * HG * HD), GROUPS * KT * HG * HD)]
                    nc.gpsimd.tensor_copy(attn_q[par][:, :, :].rearrange("p t (u c) -> p u t c", u=GROUPS),
                                          batch.rearrange("p (u h t c) -> p u h t c", u=GROUPS, h=2, t=QUAD)[:, :, par])\
                        .then_inc(attn_sorted, 1)
                if exists(1):
                    pool.wait_ge(var_done, g)
                    nc.gpsimd.tensor_tensor(rstd[:, :], var_eps[:, :], half_power[:, :], ALU.pow).then_inc(rstd_done, 1)

            nc.gpsimd.memset(half_power[:, :], -0.5).then_inc(power_set, 1)
            pool.wait_ge(power_set, 1)
            in_turn(pool, QUADS, 2, 1, quad)


def route(nc, router, load_weights, bias, before, iota_dram, gains, slots, tile_weights, carry_on):
    with ExitStack() as ctx:
        def sb(name, shape, dt=F32):
            return ctx.enter_context(nc.sbuf_tensor(name, shape, dt))

        def sem(name):
            return ctx.enter_context(nc.semaphore(name))

        N = TILES * EXPERTS
        psum = ExitStack()
        rank_ps = psum.enter_context(nc.psum_tensor("rank_ps", [P, N], F32))
        total_ps = psum.enter_context(nc.psum_tensor("total_ps", [P, N], F32))
        bias_sb = sb("bias_sb", [P, EXPERTS])
        before_sb = sb("before_sb", [P, P])
        before_b = sb("before_b", [P, P], BF16)
        ones_b = sb("ones_b", [P, P], BF16)
        falling = sb("falling", [P, EXPERTS])
        restart = sb("restart", [P, EXPERTS, TILES])
        tile_no = sb("tile_no", [P, ROUTED_TILES])
        biased = sb("biased", [P, TILES, EXPERTS])
        best = sb("best", [P, TILES])
        marks = sb("marks", [P, TILES, EXPERTS])
        chosen = sb("chosen", [P, 2, TILES, EXPERTS])
        product = sb("product", [P, 2, TILES, EXPERTS])
        score = sb("score", [P, 2, TILES])
        score_sum = sb("score_sum", [P, TILES])
        both_b = sb("both_b", [P, TILES, EXPERTS], BF16)
        total = sb("total", [P, EXPERTS, TILES])
        running = sb("running", [P, EXPERTS, TILES])
        count_i = sb("count_i", [P, EXPERTS], I32)
        tiles_of = sb("tiles_of", [P, EXPERTS])
        ends = sb("ends", [P, EXPERTS])
        starts = sb("starts", [P, EXPERTS])
        ones_e = sb("ones_e", [P, EXPERTS])
        place = sb("place", [P, TILES, EXPERTS])
        ended = sb("ended", [P, ROUTED_TILES, EXPERTS])
        expert_of = sb("expert_of", [P, ROUTED_TILES])

        loaded = sem("loaded")
        weights_loaded = sem("weights_loaded")
        step = sem("step")
        sel_ready = sem("sel_ready")
        counted = sem("counted")

        finish_step = sem("finish_step")
        tile_weights_set = sem("tile_weights_set")
        v = nc.vector

        def wide(ap):
            return ap.unsqueeze(2).broadcast_to([P, TILES, EXPERTS])

        def per_tile(ap, n=TILES):
            return ap.unsqueeze(1).broadcast_to([P, n, EXPERTS])

        scores3 = router[:, :].rearrange("p (t e) -> p t e", e=EXPERTS)
        block = psum.enter_context(nc.Block())

        @block.sync
        def _(sp):
            sp.dma_start(bias_sb[:, :], bias).then_inc(loaded, 16)
            sp.dma_start(before_sb[:, :], before).then_inc(loaded, 16)
            sp.dma_start(falling[:, :], iota_dram[:, 0:EXPERTS]).then_inc(loaded, 16)
            sp.dma_start(restart[:, :, :].rearrange("p e t -> p (e t)"), iota_dram[:, EXPERTS:EXPERTS + N]).then_inc(loaded, 16)
            sp.dma_start(tile_no[:, :], iota_dram[:, EXPERTS + N:EXPERTS + N + ROUTED_TILES]).then_inc(loaded, 16)
            load_weights(sp, weights_loaded)
            sp.wait_ge(weights_loaded, 8 * 16)

        @block.tensor
        def _(pe):
            pe.wait_ge(sel_ready, 3)
            nc.tensor.matmul(rank_ps[:, :], before_b[:, :], both_b[:, :, :].rearrange("p t e -> p (t e)"),
                             start=True, stop=True).then_inc(counted, 1)
            nc.tensor.matmul(total_ps[:, :], ones_b[:, :], both_b[:, :, :].rearrange("p t e -> p (t e)"),
                             start=True, stop=True).then_inc(counted, 1)

        @block.vector
        def _(dve):
            done = [0]

            def then(instruction):
                done[0] += 1
                instruction.then_inc(step, 1)
                dve.wait_ge(step, done[0])

            dve.wait_ge(loaded, 5 * 16)
            v.tensor_copy(before_b[:, :], before_sb[:, :]).then_inc(sel_ready, 1)
            v.memset(ones_b[:, :], 1.0).then_inc(sel_ready, 1)
            then(v.memset(ones_e[:, :], 1.0))
            then(v.tensor_tensor(biased[:, :, :], scores3, per_tile(bias_sb[:, :]), ALU.add))
            for k in range(2):
                then(v.tensor_reduce(best[:, :], biased[:, :, :], AX.X, ALU.max))
                then(v.tensor_tensor(marks[:, :, :], biased[:, :, :], wide(best[:, :]), ALU.is_equal))
                then(v.tensor_tensor(marks[:, :, :], marks[:, :, :], per_tile(falling[:, :]), ALU.mult))
                then(v.tensor_reduce(best[:, :], marks[:, :, :], AX.X, ALU.max))
                then(v.tensor_tensor(chosen[:, k, :, :], per_tile(falling[:, :]), wide(best[:, :]), ALU.is_equal))
                if k == 0:
                    then(v.scalar_tensor_tensor(biased[:, :, :], chosen[:, 0, :, :], -3.0e38, biased[:, :, :], ALU.mult, ALU.add))
            v.tensor_tensor(both_b[:, :, :], chosen[:, 0, :, :], chosen[:, 1, :, :], ALU.add).then_inc(sel_ready, 1)
            dve.wait_ge(counted, 2)
            then(v.tensor_copy(total[:, :, :], total_ps[:, :].rearrange("p (t e) -> p e t", e=EXPERTS)))
            flat = "p e t -> p (e t)"
            then(v.tensor_tensor_scan(running[:, :, :].rearrange(flat), restart[:, :, :].rearrange(flat),
                                      total[:, :, :].rearrange(flat), 0.0, ALU.mult, ALU.add))
            then(v.tensor_scalar_add(tiles_of[:, :], running[:, :, TILES - 1], float(P - 1)))
            then(v.tensor_copy(count_i[:, :], tiles_of[:, :]))
            then(v.tensor_scalar(count_i[:, :], count_i[:, :], 7, None, ALU.arith_shift_right))
            then(v.tensor_copy(tiles_of[:, :], count_i[:, :]))
            then(v.tensor_tensor_scan(ends[:, :], ones_e[:, :], tiles_of[:, :], 0.0, ALU.mult, ALU.add))
            then(v.tensor_tensor(starts[:, :], ends[:, :], tiles_of[:, :], ALU.subtract))
            then(v.tensor_scalar(starts[:, :], starts[:, :], float(P), float(T), ALU.mult, ALU.add))
            then(v.tensor_tensor(running[:, :, :], running[:, :, :], total[:, :, :], ALU.subtract))
            then(v.tensor_tensor(place[:, :, :], rank_ps[:, :].rearrange("p (t e) -> p t e", e=EXPERTS),
                                 running[:, :, :].rearrange("p e t -> p t e"), ALU.add))
            then(v.tensor_tensor(place[:, :, :], place[:, :, :], per_tile(starts[:, :]), ALU.add))
            for k in range(2):
                then(v.tensor_tensor(product[:, k, :, :], chosen[:, k, :, :], place[:, :, :], ALU.mult))
            then(v.tensor_reduce(score[:, :, :], product[:, :, :, :], AX.X, ALU.add))
            then(v.tensor_copy(slots[:, :], score[:, :, :].rearrange("p k t -> p (k t)")))

        psum.close()

        def finish(dve):
            done = [0]

            def then(instruction):
                done[0] += 1
                instruction.then_inc(finish_step, 1)
                dve.wait_ge(finish_step, done[0])

            then(v.tensor_tensor(ended[:, :, :], per_tile(ends[:, :], ROUTED_TILES),
                                 tile_no[:, :].unsqueeze(2).broadcast_to([P, ROUTED_TILES, EXPERTS]), ALU.is_le))
            then(v.tensor_reduce(expert_of[:, :], ended[:, :, :], AX.X, ALU.add))
            then(v.tensor_scalar(expert_of[:, :], expert_of[:, :], float(EXPERTS - 1), float(W_ROW), ALU.min, ALU.mult))
            v.memset(tile_weights[:, 0:TILES], EXPERTS * W_ROW).then_inc(tile_weights_set, 1)
            v.tensor_copy(tile_weights[:, TILES:ALL_TILES], expert_of[0:1, :]).then_inc(tile_weights_set, 1)
            for k in range(2):
                then(v.tensor_tensor(product[:, k, :, :], chosen[:, k, :, :], scores3, ALU.mult))
            then(v.tensor_reduce(score[:, :, :], product[:, :, :, :], AX.X, ALU.add))
            then(v.tensor_tensor(score_sum[:, :], score[:, 0, :], score[:, 1, :], ALU.add))
            then(v.tensor_scalar_add(score_sum[:, :], score_sum[:, :], 1e-20))
            then(v.reciprocal(score_sum[:, :], score_sum[:, :]))
            for k in range(2):
                then(v.tensor_tensor(gains[:, k * TILES:(k + 1) * TILES], score[:, k, :], score_sum[:, :], ALU.mult))

        carry_on(finish, tile_weights_set)


def experts(nc, eye, result_ids, weights, slots, tile_weights, rows_dram, out_dram, finish_routing, tile_weights_set):
    SLOT = 16
    N_QUADS = ALL_TILES // QUAD
    with ExitStack() as ctx:
        def sb(name, shape, dt=F32):
            return ctx.enter_context(nc.sbuf_tensor(name, shape, dt))

        def ps(name, shape, dt=F32):
            return ctx.enter_context(nc.psum_tensor(name, shape, dt))

        def sem(name):
            return ctx.enter_context(nc.semaphore(name))

        rows_t_ps = [ps(f"rows_t_ps{p}", [P, 512]) for p in range(2)]
        gate_up_ps = [ps(f"gate_up_ps{p}", [P, 512]) for p in range(2)]
        hidden_t_ps = [ps(f"hidden_t_ps{p}", [P, 512]) for p in range(2)]
        down_ps = [ps(f"down_ps{p}", [P, 512]) for p in range(2)]
        idn = sb("idn", [P, P])
        rows = [sb(f"rows{q}", [P, QUAD, ROW]) for q in range(2)]
        rows_t = [sb(f"rows_t{p}", [P, D]) for p in range(2)]
        gate = [sb(f"gate{p}", [P, F]) for p in range(2)]
        hidden = [sb(f"hidden{p}", [P, F]) for p in range(2)]
        hidden_t = [sb(f"hidden_t{p}", [P, P]) for p in range(2)]
        result = [sb(f"result{q}", [P, QUAD, D]) for q in range(2)]
        to_scatter = [sb(f"to_scatter{q}", [P, 2, QUAD, ROW]) for q in range(2)]
        result_id = sb("result_id", [P, 2 * TILES], U32)
        result_row = [sb(f"result_row{q}", [P, QUAD], U32) for q in range(2)]
        slot_q = [sb(f"slot_q{q}", [P, 2, QUAD], U32) for q in range(2)]

        idn_loaded = sem("idn_loaded")
        result_rows = sem("result_rows")
        rows_loaded = [sem(f"rows_loaded{q}") for q in range(2)]
        scatter_loaded = [sem(f"scatter_loaded{q}") for q in range(2)]
        slots_staged = sem("slots_staged")
        scattered = [sem(f"scattered{q}") for q in range(2)]
        rows_turned = sem("rows_turned")
        rows_copied = sem("rows_copied")
        gate_up_done = sem("gate_up_done")
        gate_done = sem("gate_done")
        hidden_done = sem("hidden_done")
        hidden_turned = sem("hidden_turned")
        hidden_copied = sem("hidden_copied")
        down_done = sem("down_done")
        result_copied = sem("result_copied")
        stored = [sem(f"stored{q}") for q in range(2)]
        delivered = [sem(f"delivered{q}") for q in range(2)]

        block = ctx.enter_context(nc.Block())

        def static_below(j, n):
            return isinstance(j, int) and j < n

        @block.sync
        def _(sp):
            def load(q, par, columns, routed_before):
                if routed_before:
                    wait_apart(sp, (idn_loaded, 2 * 16), (rows_turned, (q - 1) * QUAD), (result_rows, q - (QUADS + 1)))
                elif not static_below(q, 2):
                    sp.wait_ge(rows_turned, (q - 1) * QUAD)
                sp.dma_start(rows[par][:, :, 0:columns],
                             rows_dram[bass.ds(q * (QUAD * P), QUAD * P), 0:columns].rearrange("(t p) c -> p t c", p=P))\
                    .then_inc(rows_loaded[par], 16)

            def store(q, par):
                sp.wait_ge(result_copied, (q + 1) * QUAD)
                sp.dma_start(out_dram[bass.ds(q * (QUAD * P), QUAD * P), :].rearrange("(t p) c -> p t c", p=P),
                             result[par][:, :, :]).then_inc(stored[par], 16)

            def load_for_scatter(q, par):
                if not static_below(q, 2):
                    sp.wait_ge(scattered[par], (q // 2) * (2 * QUAD * 16))
                for k in range(2):
                    sp.dma_start(to_scatter[par][:, k, :, 0:D],
                                 rows_dram[bass.ds(q * (QUAD * P), QUAD * P), 0:D].rearrange("(t p) c -> p t c", p=P))\
                        .then_inc(scatter_loaded[par], 16)

            sp.dma_start(idn[:, :], eye).then_inc(idn_loaded, 16)
            sp.dma_start(result_id[:, :], result_ids).then_inc(idn_loaded, 16)
            for q in range(2):
                load(q, q, D, False)
                load_for_scatter(q, q)
            with sp.Fori(1, QUADS // 2) as i:
                for par in range(2):
                    load(i * 2 + par, par, D, False)
                    load_for_scatter(i * 2 + par, par)
                    store(i * 2 + (par - 2), par)
            store(QUADS - 2, 0)
            for par in range(2):
                sp.wait_ge(scattered[par], QUADS // 2 * (2 * QUAD * 16))
            for par in range(2):
                load(QUADS + par, par, ROW, False)
            store(QUADS - 1, 1)
            with sp.Fori(QUADS // 2 + 1, N_QUADS // 2) as i:
                for par in range(2):
                    load(i * 2 + par, par, ROW, True)
            for par in range(2):
                sp.wait_ge(stored[par], QUADS // 2 * 16)

        @block.gpsimd
        def _(pool):
            def scatter(q, par, exists):
                if not static_below(q, 2):
                    wait_apart(pool, (idn_loaded, 2 * 16), (scattered[par], (q // 2) * (2 * QUAD * 16)))
                nc.gpsimd.tensor_copy(slot_q[par][:, :, :], slots[:, :].rearrange("p (k t) -> p k t", k=2)[:, :, bass.ds(q * QUAD, QUAD)])\
                    .then_inc(slots_staged, 1)
                nc.gpsimd.tensor_copy(to_scatter[par][:, :, :, :].bitcast(U32)[:, :, :, D],
                                      result_id[:, :].rearrange("p (k t) -> p k t", k=2)[:, :, bass.ds(q * QUAD, QUAD)])\
                    .then_inc(slots_staged, 1)
                wait_apart(pool, (idn_loaded, 2 * 16), (slots_staged, q * 2 + 2), (scatter_loaded[par], (q // 2 + 1) * 32))
                for t in range(QUAD):
                    for k in range(2):
                        nc.gpsimd.indirect_dma_start(rows_dram, bass.IndirectOffsetOnAxis(slot_q[par][:, k, t:t + 1], 0),
                                                     to_scatter[par][:, k, t, :], None).then_inc(scattered[par], 16)

            def take_result_rows(q, par):
                waits = [(rows_loaded[par], (q // 2 + 1) * 16)]
                if not static_below(q, QUADS + 2):
                    waits.append((delivered[par], (q - par) * (QUAD * 16 // 2) - QUADS // 2 * (QUAD * 16)))
                wait_apart(pool, (idn_loaded, 2 * 16), *waits)
                nc.gpsimd.tensor_copy(result_row[par][:, :], rows[par][:, :, :].bitcast(U32)[:, :, D]).then_inc(result_rows, 1)

            def deliver(q, par, more):
                for t in range(QUAD):
                    wait_apart(pool, (idn_loaded, 2 * 16), (result_rows, q - (QUADS - 1)), (result_copied, q * QUAD + (t + 1)))
                    nc.gpsimd.indirect_dma_start(out_dram, bass.IndirectOffsetOnAxis(result_row[par][:, t:t + 1], 0),
                                                 result[par][:, t, :], None).then_inc(delivered[par], 16)
                    if t == 1 and more:
                        take_result_rows(q + 1, 1 - par)

            pool.wait_ge(idn_loaded, 2 * 16)
            in_turn(pool, QUADS, 2, 0, scatter)
            take_result_rows(QUADS, 0)
            deliver(QUADS, 0, True)
            with pool.Fori(0, (N_QUADS - QUADS) // 2 - 1) as i:
                deliver(i * 2 + (QUADS + 1), 1, True)
                deliver(i * 2 + (QUADS + 2), 0, True)
            deliver(N_QUADS - 1, 1, False)
            for par in range(2):
                pool.wait_ge(scattered[par], QUADS // 2 * (2 * QUAD * 16))
                pool.wait_ge(delivered[par], (N_QUADS - QUADS) // 2 * (QUAD * 16))

        @block.tensor
        def _(pe):
            held = {}

            def starts_of(j, k, back):
                if (k - back) % SLOT not in held:
                    held[(k - back) % SLOT] = pe.value_load(tile_weights[0:1, bass.ds(j - back, 1)], min_val=0, max_val=EXPERTS * W_ROW)
                return held[(k - back) % SLOT]

            def tile(j, k, exists):
                if k == 0:
                    held.clear()
                held.pop((k - 4) % SLOT, None)
                if exists(0):
                    q = k // QUAD % 2
                    if k % QUAD == 0:
                        pe.wait_ge(rows_loaded[q], (j - k) * (16 // (2 * QUAD)) + (k // (2 * QUAD) + 1) * 16)
                    if not static_below(j, 2):
                        pe.wait_ge(rows_copied, j - 1)
                    for c in range(2):
                        last = nc.tensor.transpose(rows_t_ps[k % 2][:, c * P:(c + 1) * P], rows[q][:, k % QUAD, c * P:(c + 1) * P], idn[:, :])
                    last.then_inc(rows_turned, 1)
                if exists(1):
                    n = (k - 1) % 2
                    at = starts_of(j, k, 1)
                    pe.wait_ge(rows_copied, j)
                    if not static_below(j, 3):
                        pe.wait_ge(hidden_done, j - 2)
                    for c in range(2):
                        last = nc.tensor.matmul(gate_up_ps[n][:, 0:2 * F], rows_t[n][:, c * P:(c + 1) * P],
                                                weights[:, bass.ds(at + c * 2 * F, 2 * F)], start=(c == 0), stop=(c == 1))
                    last.then_inc(gate_up_done, 1)
                if exists(0):
                    starts_of(j, k, 0)
                if exists(2):
                    n = k % 2
                    pe.wait_ge(hidden_done, j - 1)
                    if not static_below(j, 4):
                        pe.wait_ge(hidden_copied, j - 3)
                    nc.tensor.transpose(hidden_t_ps[n][:, 0:P], hidden[n][:, :], idn[:, :]).then_inc(hidden_turned, 1)
                if exists(3):
                    n = (k - 1) % 2
                    at = starts_of(j, k, 3)
                    pe.wait_ge(hidden_copied, j - 2)
                    if not static_below(j, 5):
                        pe.wait_ge(result_copied, j - 4)
                    nc.tensor.matmul(down_ps[n][:, 0:D], hidden_t[n][:, :], weights[:, bass.ds(at + 4 * F, D)],
                                     start=True, stop=True).then_inc(down_done, 1)

            pe.wait_ge(idn_loaded, 2 * 16)
            pe.wait_ge(tile_weights_set, 2)
            in_turn(pe, ALL_TILES, SLOT, 3, tile)

        @block.scalar
        def _(act):
            def tile(j, k, exists):
                if exists(1):
                    n = (k - 1) % 2
                    act.wait_ge(gate_up_done, j)
                    if not static_below(j, 3):
                        act.wait_ge(hidden_done, j - 2)
                    nc.scalar.activation(gate[n][:, :], gate_up_ps[n][:, 0:F], ACT.Silu).then_inc(gate_done, 1)
                if exists(3):
                    n, r = (k - 1) % 2, (k - 3) % SLOT
                    act.wait_ge(down_done, j - 2)
                    if r % QUAD == 0:
                        q = (j - 3) // QUAD if isinstance(j, int) else None
                        if q is None:
                            act.wait_ge(delivered[r // QUAD % 2],
                                        (j - k) * (QUAD * 16 // (2 * QUAD)) + (r // (2 * QUAD) * (QUAD * 16) - QUADS // 2 * (QUAD * 16)))
                        elif q >= QUADS + 2:
                            act.wait_ge(delivered[q % 2], (q - QUADS) // 2 * (QUAD * 16))
                        elif q >= 2:
                            act.wait_ge(stored[q % 2], q // 2 * 16)
                    nc.scalar.copy(result[r // QUAD % 2][:, r % QUAD, :], down_ps[n][:, 0:D]).then_inc(result_copied, 1)

            in_turn(act, ALL_TILES, SLOT, 3, tile, TILES // SLOT + 1)

        @block.vector
        def _(dve):
            def tile(j, k, exists):
                if exists(0):
                    dve.wait_ge(rows_turned, j + 1)
                    if not static_below(j, 2):
                        dve.wait_ge(gate_up_done, j - 1)
                    nc.vector.tensor_copy(rows_t[k % 2][:, :], rows_t_ps[k % 2][:, 0:D]).then_inc(rows_copied, 1)
                if exists(1):
                    n = (k - 1) % 2
                    dve.wait_ge(gate_done, j)
                    if not static_below(j, 3):
                        dve.wait_ge(hidden_turned, j - 2)
                    nc.vector.tensor_tensor(hidden[n][:, :], gate_up_ps[n][:, F:2 * F], gate[n][:, :], ALU.mult).then_inc(hidden_done, 1)
                if exists(2):
                    n = k % 2
                    dve.wait_ge(hidden_turned, j - 1)
                    if not static_below(j, 4):
                        dve.wait_ge(down_done, j - 3)
                    nc.vector.tensor_copy(hidden_t[n][:, :], hidden_t_ps[n][:, 0:P]).then_inc(hidden_copied, 1)

            finish_routing(dve)
            in_turn(dve, ALL_TILES, SLOT, 2, tile)


def combine(nc, gains, rows_dram, out_dram, out):
    DEEP = 4
    with ExitStack() as ctx:
        def sb(name, shape, dt=F32):
            return ctx.enter_context(nc.sbuf_tensor(name, shape, dt))

        def sem(name):
            return ctx.enter_context(nc.semaphore(name))

        minus_half = sb("minus_half", [P, QUAD])
        routed = [sb(f"routed{q}", [P, 2, QUAD, D]) for q in range(DEEP)]
        x1_g = [sb(f"x1_g{q}", [P, QUAD, D]) for q in range(DEEP)]
        shared_g = [sb(f"shared_g{q}", [P, QUAD, D]) for q in range(DEEP)]
        total_g = [sb(f"total_g{q}", [P, QUAD, D]) for q in range(DEEP)]
        stats_g = sb("stats_g", [P, QUAD, 6])
        meanvar_g = [sb(f"meanvar_g{q}", [P, QUAD, 2]) for q in range(DEEP)]
        var_g = sb("var_g", [P, QUAD])
        rstd_g = sb("rstd_g", [P, QUAD])
        shift_g = sb("shift_g", [P, QUAD])
        normed = [sb(f"normed{q}", [P, QUAD, D]) for q in range(DEEP)]

        half_set = sem("half_set")
        fetched = [sem(f"fetched{q}") for q in range(DEEP)]
        first_added = sem("first_added")
        second_added = sem("second_added")
        shared_added = sem("shared_added")
        stats_g_done = sem("stats_g_done")
        meanvar_g_done = sem("meanvar_g_done")
        var_g_done = sem("var_g_done")
        rstd_g_done = sem("rstd_g_done")
        shift_done = sem("shift_done")
        normed_done = sem("normed_done")
        out_stored = [sem(f"out_stored{q}") for q in range(DEEP)]

        block = ctx.enter_context(nc.Block())

        def static_below(j, n):
            return isinstance(j, int) and j < n

        def rows_of(dram, q):
            return dram[bass.ds(q * (QUAD * P), QUAD * P), :].rearrange("(t p) c -> p t c", p=P)

        @block.sync
        def _(sp):
            def quad(q, par, exists):
                if exists(0):
                    if not static_below(q, DEEP):
                        sp.wait_ge(second_added, (q - (DEEP - 1)) * QUAD)
                    sp.dma_start(x1_g[par][:, :, :], rows_of(rows_dram[:, 0:D], q)).then_inc(fetched[par], 16)
                    for k in range(2):
                        sp.dma_start(routed[par][:, k, :, :], rows_of(out_dram, q + (k + 1) * QUADS)).then_inc(fetched[par], 16)
                    sp.dma_start(shared_g[par][:, :, :], rows_of(out_dram, q)).then_inc(fetched[par], 16)

            in_turn(sp, QUADS, DEEP, 0, quad)

        @block.gpsimd
        def _(pool):
            def quad(q, par, exists):
                if exists(0):
                    pool.wait_ge(fetched[par], (q // DEEP + 1) * (4 * 16))
                    if not static_below(q, DEEP):
                        pool.wait_ge(normed_done, q - (DEEP - 1))
                    nc.gpsimd.tensor_tensor(total_g[par][:, :, :], x1_g[par][:, :, :], shared_g[par][:, :, :], ALU.add)\
                        .then_inc(shared_added, 1)
                if exists(1):
                    pool.wait_ge(var_g_done, q)
                    if not static_below(q, 2):
                        pool.wait_ge(normed_done, q - 1)
                    nc.gpsimd.tensor_tensor(rstd_g[:, :], var_g[:, :], minus_half[:, :], ALU.pow).then_inc(rstd_g_done, 1)

            nc.gpsimd.memset(minus_half[:, :], -0.5).then_inc(half_set, 1)
            pool.wait_ge(half_set, 1)
            in_turn(pool, QUADS, DEEP, 1, quad)

        @block.vector
        def _(dve):
            def quad(q, par, exists):
                if exists(0):
                    dve.wait_ge(fetched[par], (q // DEEP + 1) * (4 * 16))
                    dve.wait_ge(shared_added, q + 1)
                    for t in range(QUAD):
                        nc.vector.scalar_tensor_tensor(total_g[par][:, t, :], routed[par][:, 0, t, :], gains[:, bass.ds(q * QUAD + t, 1)],
                                                       total_g[par][:, t, :], ALU.mult, ALU.add).then_inc(first_added, 1)
                    for t in range(QUAD):
                        dve.wait_ge(first_added, q * QUAD + (t + 1))
                        nc.vector.scalar_tensor_tensor(total_g[par][:, t, :], routed[par][:, 1, t, :],
                                                       gains[:, bass.ds(q * QUAD + (TILES + t), 1)],
                                                       total_g[par][:, t, :], ALU.mult, ALU.add).then_inc(second_added, 1)
                    dve.wait_ge(second_added, q * QUAD + QUAD)
                    for t in range(QUAD):
                        nc.vector.bn_stats(stats_g[:, t, :], total_g[par][:, t, :]).then_inc(stats_g_done, 1)
                if exists(1):
                    dve.wait_ge(rstd_g_done, q)
                    if not static_below(q, 2):
                        dve.wait_ge(normed_done, q - 1)
                    nc.vector.scalar_tensor_tensor(shift_g[:, :], meanvar_g[(par - 1) % DEEP][:, :, 0], -1.0, rstd_g[:, :],
                                                   ALU.mult, ALU.mult).then_inc(shift_done, 1)
                if exists(0):
                    for t in range(QUAD):
                        wait_apart(dve, (half_set, 1), (stats_g_done, q * QUAD + (t + 1)))
                        nc.vector.bn_aggr(meanvar_g[par][:, t, :], stats_g[:, t, :]).then_inc(meanvar_g_done, 1)
                    dve.wait_ge(meanvar_g_done, q * QUAD + QUAD)
                    nc.vector.tensor_scalar_add(var_g[:, :], meanvar_g[par][:, :, 1], EPS).then_inc(var_g_done, 1)

            in_turn(dve, QUADS, DEEP, 1, quad)

        @block.scalar
        def _(act):
            def quad(q, par, exists):
                if exists(0):
                    act.wait_ge(shift_done, q + 1)
                    if not static_below(q, DEEP):
                        act.wait_ge(out_stored[par], q // DEEP * 16)
                    for t in range(QUAD):
                        last = nc.scalar.activation(normed[par][:, t, :], total_g[par][:, t, :], ACT.Identity,
                                                    bias=shift_g[:, t:t + 1], scale=rstd_g[:, t:t + 1])
                    last.then_inc(normed_done, 1)
                if exists(1):
                    before = (par - 1) % DEEP
                    act.wait_ge(normed_done, q)
                    act.dma_start(rows_of(out, q - 1), normed[before][:, :, :]).then_inc(out_stored[before], 16)

            in_turn(act, QUADS, DEEP, 1, quad)
            for par in range(DEEP):
                act.wait_ge(out_stored[par], QUADS // DEEP * 16)


def transformer_block(nc, x, x_t, w_units, w_proj, gate_w, bias, shared_gate, shared_up, shared_down, gate_up, down,
                      cos_t, sin_t, eye, before, integers, spare_ids, result_ids, out):
    parts_dram = nc.dram_tensor("parts_dram", (UNITS, 2, PARTS, HD, 2, HG, HALF), BF16, kind="Internal").ap()
    rows_dram = nc.dram_tensor("rows_dram", (ALL_TILES * P, ROW), F32, kind="Internal").ap()
    out_dram = nc.dram_tensor("out_dram", (3 * T + ROUTED_TILES * P, D), F32, kind="Internal").ap()

    with ExitStack() as ctx:
        def sb(name, shape, dt=F32):
            return ctx.enter_context(nc.sbuf_tensor(name, shape, dt))

        router = sb("router", [P, TILES * EXPERTS])
        gains = sb("gains", [P, 2 * TILES])
        slots = sb("slots", [P, 2 * TILES], U32)
        tile_weights = sb("tile_weights", [1, ALL_TILES], I32)
        weights = sb("weights", [P, (EXPERTS + 1) * W_ROW])
        with nc.sbuf_tensor("attn", [P, UNITS * KT * HG * HD], F32) as attn:
            attention(nc, x_t, w_units, cos_t, sin_t, eye, parts_dram, attn, rows_dram, spare_ids)
            attention_norm_router(nc, x, w_proj, gate_w, eye, attn, rows_dram, router)
        def load_weights(engine, signal):
            w3 = weights[:, :].rearrange("p (e n) -> p e n", n=W_ROW)
            for c in range(2):
                engine.dma_start(w3[:, 0:EXPERTS, c * 2 * F:(c + 1) * 2 * F],
                                 gate_up[:, c * P:(c + 1) * P, :].rearrange("e p n -> p e n")).then_inc(signal, 16)
                engine.dma_start(w3[:, EXPERTS, c * 2 * F:c * 2 * F + F], shared_gate[c * P:(c + 1) * P, :]).then_inc(signal, 16)
                engine.dma_start(w3[:, EXPERTS, c * 2 * F + F:(c + 1) * 2 * F], shared_up[c * P:(c + 1) * P, :]).then_inc(signal, 16)
            engine.dma_start(w3[:, 0:EXPERTS, 4 * F:4 * F + D], down.rearrange("e p n -> p e n")).then_inc(signal, 16)
            engine.dma_start(w3[:, EXPERTS, 4 * F:4 * F + D], shared_down).then_inc(signal, 16)
        route(nc, router, load_weights, bias, before, integers, gains, slots, tile_weights,
              lambda finish, tile_weights_set: experts(nc, eye, result_ids, weights, slots, tile_weights, rows_dram, out_dram,
                                                       finish, tile_weights_set))
        combine(nc, gains, rows_dram, out_dram, out)


def _constants():
    import numpy as np

    freqs = np.float32(1.0) / np.float32(10000.0) ** (np.arange(0, HD, 2, dtype=np.float32) / np.float32(HD))
    angles = np.outer(np.arange(L, dtype=np.float32), freqs).astype(np.float32)
    cos = np.repeat(np.cos(angles), 2, axis=-1).T
    sin = np.repeat(np.sin(angles), 2, axis=-1).T.copy()
    sin[0::2] *= -1
    falling = np.arange(EXPERTS, 0, -1, dtype=np.float32)
    restart = np.tile((np.arange(TILES) > 0).astype(np.float32), EXPERTS)
    tile_no = np.arange(ROUTED_TILES, dtype=np.float32)
    integers = np.concatenate([falling, restart, tile_no])
    slot = np.arange(ROUTED_TILES * P, dtype=np.uint32).reshape(-1, P, BLANK).transpose(1, 0, 2).reshape(P, -1)
    token = np.arange(T, dtype=np.uint32).reshape(TILES, P).T
    return {
        "spare_ids": slot + np.uint32(3 * T),
        "result_ids": np.concatenate([token + np.uint32(T), token + np.uint32(2 * T)], axis=1),
        "cos_t": np.tile(cos, (2 * HG, 1)).astype(np.float32),
        "sin_t": np.tile(sin, (2 * HG, 1)).astype(np.float32),
        "eye": np.eye(P, dtype=np.float32),
        "before": np.triu(np.ones((P, P), np.float32), 1),
        "integers": np.ascontiguousarray(np.broadcast_to(integers, (P, integers.size))),
    }


def kernel(**inputs):
    import concourse.bacc as bacc
    import numpy as np
    from concourse.bass_utils import run_bass_kernel_spmd

    a = {name: np.asarray(value) for name, value in inputs.items()}
    x = a["L0_attn_x"]
    arrays = {
        "x": x.reshape(T, D),
        "x_t": x.transpose(0, 2, 1),
        "w_units": a["L0_attn_w_qkv"].reshape(D, 3, GROUPS, HG * HD).transpose(2, 0, 1, 3).reshape(GROUPS, D, 3 * HG * HD),
        "w_proj": a["L0_attn_w_proj"],
        "gate_w": a["L0_ffn_gate_w"],
        "bias": np.broadcast_to(a["L0_ffn_expert_bias"], (P, EXPERTS)),
        "shared_gate": a["L0_ffn_shared_gate_w"],
        "shared_up": a["L0_ffn_shared_up_w"],
        "shared_down": a["L0_ffn_shared_down_w"],
        "gate_up": a["L0_ffn_experts_gate_up"],
        "down": a["L0_ffn_experts_down"],
        **_constants(),
    }
    arrays = {name: np.ascontiguousarray(value) for name, value in arrays.items()}
    nc = bacc.Bacc("TRN2", target_bir_lowering=False, num_devices=1)
    args = {name: nc.dram_tensor(f"in_{name}", value.shape, mybir.dt.from_np(value.dtype), kind="ExternalInput").ap()
            for name, value in arrays.items()}
    out = nc.dram_tensor("out_0", (T, D), F32, kind="ExternalOutput").ap()
    transformer_block(nc, **args, out=out)
    result = run_bass_kernel_spmd(nc, [{f"in_{name}": value for name, value in arrays.items()}], core_ids=[0])
    return result.results[0]["out_0"].reshape(B, L, D)
```
